# Optimizing a Trainium2 kernel written in Bass

```python
import numpy as np
import jax
import jax.numpy as jnp

def _softmax(x, axis=-1):
    return jax.nn.softmax(x, axis=axis)

def _gelu(x):
    return jax.nn.gelu(x, approximate=True)

def _silu(x):
    return jax.nn.silu(x)

def _sigmoid(x):
    return jax.nn.sigmoid(x)

def _layernorm(x, axis=-1, eps=1e-05):
    m = jnp.mean(x, axis=axis, keepdims=True)
    v = jnp.var(x, axis=axis, keepdims=True)
    return (x - m) / jnp.sqrt(v + eps)

def _scatter_add(tgt, idx, src, axis=0):
    return tgt.at[idx].add(src)

def _segment_sum(src, seg, n):
    return jax.ops.segment_sum(src, seg, n)
kernel_name = 'mk_lm_tower_d1_tok_ids4096_r4_dd9431'

def setup_inputs(seed: int=0):
    np.random.seed(seed)
    _w = jnp.asarray

    def _rec_inputs():
        import jax
        import jax.numpy as jnp
        _rk = jax.random.key(seed)
        x = jax.random.randint(jax.random.fold_in(_rk, 1), (2, 2048), 0, 1024, jnp.int32)
        return x
    x = _rec_inputs()

    def _L0_tok_setup():
        import jax, jax.numpy as jnp
        import numpy as np
        V = 1024
        M = 4
        B = 8
        L = 512

        def _contexts(idx, vocab, order):
            Bb, Ll = idx.shape
            cols = []
            for k in range(order):
                s = order - 1 - k
                if s == 0:
                    cols.append(idx)
                else:
                    pad = jnp.full((Bb, s), vocab, dtype=idx.dtype)
                    cols.append(jnp.concatenate([pad, idx[:, :Ll - s]], axis=1))
            return jnp.stack(cols, axis=-1)
        key = jax.random.key(seed)
        k1, k2 = jax.random.split(key, 2)
        idx = jax.random.randint(k1, (B, L), 0, V, dtype=jnp.int64 if jax.config.jax_enable_x64 else jnp.int32)
        fan_in = M * (V + 1)
        bound = 1.0 / np.sqrt(fan_in)
        W = jax.random.uniform(k2, (V, fan_in), minval=-bound, maxval=bound, dtype=jnp.float32)
        b = jax.random.uniform(jax.random.fold_in(k2, 1), (V,), minval=-bound, maxval=bound, dtype=jnp.float32)
        return {'idx': idx, 'W': W, 'b': b}
    _L0_tok_all = _L0_tok_setup()
    _L0_tok_in = {k: v for k, v in _L0_tok_all.items() if k in ('W', 'b')}
    del _L0_tok_all

    def _L0_attn_setup():
        import jax, jax.numpy as jnp
        import numpy as np
        import math
        D_MODEL = 1024
        NUM_HEADS = 32
        NUM_KV_HEADS = 8
        HEAD_DIM = D_MODEL // NUM_HEADS
        GROUP = NUM_HEADS // NUM_KV_HEADS
        SEQ_LEN = 512
        BATCH = 2
        ROPE_THETA = 10000.0

        def apply_rope(x, start_pos=0):
            b, h, s, hd = x.shape
            inv_freq = 1.0 / ROPE_THETA ** (jnp.arange(0, hd, 2, dtype=jnp.float32) / hd)
            pos = jnp.arange(start_pos, start_pos + s, dtype=jnp.float32)
            ang = pos[:, None] * inv_freq[None, :]
            cos = jnp.cos(ang).astype(x.dtype)
            sin = jnp.sin(ang).astype(x.dtype)
            xr = x[..., 0::2]
            xi = x[..., 1::2]
            out_r = xr * cos - xi * sin
            out_i = xr * sin + xi * cos
            return jnp.stack([out_r, out_i], axis=-1).reshape(b, h, s, hd)
        key = jax.random.key(seed)
        ks = jax.random.split(key, 5)
        qkv_dim = HEAD_DIM * (NUM_HEADS + 2 * NUM_KV_HEADS)
        scale = 1.0 / math.sqrt(D_MODEL)
        return {'x': jax.random.normal(ks[0], (BATCH, SEQ_LEN, D_MODEL), jnp.float32), 'w_qkv': jax.random.normal(ks[1], (qkv_dim, D_MODEL), jnp.float32) * scale, 'b_qkv': jax.random.normal(ks[2], (qkv_dim,), jnp.float32) * 0.01, 'w_o': jax.random.normal(ks[3], (D_MODEL, D_MODEL), jnp.float32) * scale, 'b_o': jax.random.normal(ks[4], (D_MODEL,), jnp.float32) * 0.01}
    _L0_attn_all = _L0_attn_setup()
    _L0_attn_in = {k: v for k, v in _L0_attn_all.items() if k in ('w_qkv', 'b_qkv', 'w_o', 'b_o')}
    del _L0_attn_all

    def _L0_ffn_setup():
        import math
        import jax, jax.numpy as jnp
        import numpy as np
        SCALING = 16.0 / 32.0

        def real_fourier_orthogonal_multiply(c):
            n = c.shape[-1]
            sqrt_n = math.sqrt(n)
            pair_scale = math.sqrt(n / 2.0)
            max_f = (n - 1) // 2
            work = c.astype(jnp.float32)
            dc = (work[..., 0] * sqrt_n)[..., None].astype(jnp.complex64)
            cos = work[..., 1:1 + 2 * max_f:2] * pair_scale
            sin = work[..., 2:2 + 2 * max_f:2] * pair_scale
            mid = (cos - 1j * sin).astype(jnp.complex64)
            parts = [dc, mid]
            if n % 2 == 0:
                parts.append((work[..., -1] * sqrt_n)[..., None].astype(jnp.complex64))
            spectrum = jnp.concatenate(parts, axis=-1)
            return jnp.fft.irfft(spectrum, n=n, axis=-1).astype(c.dtype)
        key = jax.random.key(seed)
        ks = jax.random.split(key, 9)
        B, S, D_in, D_out, R0, R1, E = (4, 512, 1024, 1024, 32, 8, 3)
        x = jax.random.normal(ks[0], (B, S, D_in), dtype=jnp.float32)
        W_base = jax.random.normal(ks[1], (D_out, D_in), dtype=jnp.float32) * 0.02
        b_base = jax.random.normal(ks[2], (D_out,), dtype=jnp.float32) * 0.02
        enc0 = jax.random.normal(ks[3], (R0, D_in), dtype=jnp.float32) * 0.02
        enc1 = jax.random.normal(ks[4], (R1, D_in), dtype=jnp.float32) * 0.02
        coefs0 = jax.random.normal(ks[5], (E, D_out, R0), dtype=jnp.float32) * 0.02
        coefs1 = jax.random.normal(ks[6], (E, D_out, R1), dtype=jnp.float32) * 0.02
        mask0 = jax.random.randint(ks[7], (E, D_out, R0), 0, 2).astype(bool)
        mask1 = jax.random.randint(ks[8], (E, D_out, R1), 0, 2).astype(bool)
        return dict(x=x, W_base=W_base, b_base=b_base, enc0=enc0, enc1=enc1, coefs0=coefs0, coefs1=coefs1, mask0=mask0, mask1=mask1)
    _L0_ffn_all = _L0_ffn_setup()
    _L0_ffn_in = {k: v for k, v in _L0_ffn_all.items() if k in ('W_base', 'b_base', 'enc0', 'enc1', 'coefs0', 'coefs1', 'mask0', 'mask1')}
    del _L0_ffn_all
    return {'x': x, 'L0_tok_W': _L0_tok_in['W'], 'L0_tok_b': _L0_tok_in['b'], 'L0_attn_w_qkv': _L0_attn_in['w_qkv'], 'L0_attn_b_qkv': _L0_attn_in['b_qkv'], 'L0_attn_w_o': _L0_attn_in['w_o'], 'L0_attn_b_o': _L0_attn_in['b_o'], 'L0_ffn_W_base': _L0_ffn_in['W_base'], 'L0_ffn_b_base': _L0_ffn_in['b_base'], 'L0_ffn_enc0': _L0_ffn_in['enc0'], 'L0_ffn_enc1': _L0_ffn_in['enc1'], 'L0_ffn_coefs0': _L0_ffn_in['coefs0'], 'L0_ffn_coefs1': _L0_ffn_in['coefs1'], 'L0_ffn_mask0': _L0_ffn_in['mask0'], 'L0_ffn_mask1': _L0_ffn_in['mask1']}

def reference(x, L0_tok_W, L0_tok_b, L0_attn_w_qkv, L0_attn_b_qkv, L0_attn_w_o, L0_attn_b_o, L0_ffn_W_base, L0_ffn_b_base, L0_ffn_enc0, L0_ffn_enc1, L0_ffn_coefs0, L0_ffn_coefs1, L0_ffn_mask0, L0_ffn_mask1):
    import jax
    import jax.numpy as jnp

    def _L0_tok_ref(idx, W, b):
        import jax, jax.numpy as jnp
        import numpy as np
        V = 1024
        M = 4
        B = 8
        L = 512

        def _contexts(idx, vocab, order):
            Bb, Ll = idx.shape
            cols = []
            for k in range(order):
                s = order - 1 - k
                if s == 0:
                    cols.append(idx)
                else:
                    pad = jnp.full((Bb, s), vocab, dtype=idx.dtype)
                    cols.append(jnp.concatenate([pad, idx[:, :Ll - s]], axis=1))
            return jnp.stack(cols, axis=-1)
        vocab = W.shape[0]
        order = W.shape[1] // (vocab + 1)
        x = _contexts(idx, vocab, order)
        Wt = W.T.reshape(order, vocab + 1, vocab)
        logits = b
        for k in range(order):
            logits = logits + Wt[k][x[..., k]]
        return logits

    def _L0_attn_ref(x, w_qkv, b_qkv, w_o, b_o):
        import jax, jax.numpy as jnp
        import numpy as np
        import math
        D_MODEL = 1024
        NUM_HEADS = 32
        NUM_KV_HEADS = 8
        HEAD_DIM = D_MODEL // NUM_HEADS
        GROUP = NUM_HEADS // NUM_KV_HEADS
        SEQ_LEN = 512
        BATCH = 2
        ROPE_THETA = 10000.0

        def apply_rope(x, start_pos=0):
            b, h, s, hd = x.shape
            inv_freq = 1.0 / ROPE_THETA ** (jnp.arange(0, hd, 2, dtype=jnp.float32) / hd)
            pos = jnp.arange(start_pos, start_pos + s, dtype=jnp.float32)
            ang = pos[:, None] * inv_freq[None, :]
            cos = jnp.cos(ang).astype(x.dtype)
            sin = jnp.sin(ang).astype(x.dtype)
            xr = x[..., 0::2]
            xi = x[..., 1::2]
            out_r = xr * cos - xi * sin
            out_i = xr * sin + xi * cos
            return jnp.stack([out_r, out_i], axis=-1).reshape(b, h, s, hd)
        bs, seq_len, d_model = x.shape
        qkv = x @ w_qkv.T + b_qkv
        q_dim = NUM_HEADS * HEAD_DIM
        kv_dim = NUM_KV_HEADS * HEAD_DIM
        q, k, v = jnp.split(qkv, [q_dim, q_dim + kv_dim], axis=-1)
        q = q.reshape(bs, seq_len, NUM_HEADS, HEAD_DIM).transpose(0, 2, 1, 3)
        k = k.reshape(bs, seq_len, NUM_KV_HEADS, HEAD_DIM).transpose(0, 2, 1, 3)
        v = v.reshape(bs, seq_len, NUM_KV_HEADS, HEAD_DIM).transpose(0, 2, 1, 3)
        q = apply_rope(q, 0)
        k = apply_rope(k, 0)
        k = jnp.repeat(k, GROUP, axis=1)
        v = jnp.repeat(v, GROUP, axis=1)
        scores = jnp.einsum('bhqd,bhkd->bhqk', q, k) / math.sqrt(HEAD_DIM)
        causal = jnp.tril(jnp.ones((seq_len, seq_len), dtype=bool))
        scores = jnp.where(causal[None, None, :, :], scores, jnp.float32(-1e+20))
        attn = jax.nn.softmax(scores, axis=-1)
        out = jnp.einsum('bhqk,bhkd->bhqd', attn, v)
        out = out.transpose(0, 2, 1, 3).reshape(bs, seq_len, d_model)
        return out @ w_o.T + b_o

    def _L0_ffn_ref(x, W_base, b_base, enc0, enc1, coefs0, coefs1, mask0, mask1):
        import math
        import jax, jax.numpy as jnp
        import numpy as np
        SCALING = 16.0 / 32.0

        def real_fourier_orthogonal_multiply(c):
            n = c.shape[-1]
            sqrt_n = math.sqrt(n)
            pair_scale = math.sqrt(n / 2.0)
            max_f = (n - 1) // 2
            work = c.astype(jnp.float32)
            dc = (work[..., 0] * sqrt_n)[..., None].astype(jnp.complex64)
            cos = work[..., 1:1 + 2 * max_f:2] * pair_scale
            sin = work[..., 2:2 + 2 * max_f:2] * pair_scale
            mid = (cos - 1j * sin).astype(jnp.complex64)
            parts = [dc, mid]
            if n % 2 == 0:
                parts.append((work[..., -1] * sqrt_n)[..., None].astype(jnp.complex64))
            spectrum = jnp.concatenate(parts, axis=-1)
            return jnp.fft.irfft(spectrum, n=n, axis=-1).astype(c.dtype)
        base = jnp.einsum('bsd,od->bso', x, W_base) + b_base
        e0 = jnp.einsum('bsd,rd->bsr', x, enc0)
        e1 = jnp.einsum('bsd,rd->bsr', x, enc1)
        w0 = coefs0 * mask0.astype(coefs0.dtype)
        w1 = coefs1 * mask1.astype(coefs1.dtype)
        decoded = jnp.einsum('bsr,eor->ebso', e0, w0) + jnp.einsum('bsr,eor->ebso', e1, w1)
        transformed = real_fourier_orthogonal_multiply(decoded)
        update = transformed.sum(axis=0)
        return base + update * SCALING
    h = _L0_tok_ref(x, L0_tok_W, L0_tok_b)
    h = h + _L0_attn_ref(_layernorm(h, axis=-1), L0_attn_w_qkv, L0_attn_b_qkv, L0_attn_w_o, L0_attn_b_o)
    h = h + _L0_ffn_ref(_layernorm(h, axis=-1), L0_ffn_W_base, L0_ffn_b_base, L0_ffn_enc0, L0_ffn_enc1, L0_ffn_coefs0, L0_ffn_coefs1, L0_ffn_mask0, L0_ffn_mask1)
    return h

_drawn_inputs = setup_inputs


def setup_inputs(seed=0):
    import zlib

    import numpy as np

    out = dict(_drawn_inputs(seed))
    spreads = {}
    factors = {}
    for name, (base, spread) in spreads.items():
        noise = np.random.default_rng([zlib.crc32(name.encode()), seed]).standard_normal(out[name].shape)
        drawn = base * np.exp(spread * noise) if base else spread * noise
        out[name] = jnp.asarray(drawn.astype(out[name].dtype))
    for name, factor in factors.items():
        out[name] = (out[name] * factor).astype(out[name].dtype)
    return out
```

```python
from contextlib import ExitStack

import numpy as np

import concourse.bass as bass
from concourse import mybir

P = 128
F32 = mybir.dt.float32
F32R = mybir.dt.float32r
I32 = mybir.dt.int32
U8 = mybir.dt.uint8
ALU = mybir.AluOpType
ACT = mybir.ActivationFunctionType
AX = mybir.AxisListType.X

BATCH, SEQ, D, VOCAB, ORDER = 2, 2048, 1024, 1024, 4
HEADS, KV_HEADS, HD = 32, 8, 32
GROUP = HEADS // KV_HEADS
Q_DIM, KV_DIM = HEADS * HD, KV_HEADS * HD
QKV_DIM = Q_DIM + 2 * KV_DIM
EPS = 1e-5
R0, R1, E = 32, 8, 3
R = R0 + R1
SCALING = 16.0 / 32.0
DC = D // P
TOKENS = BATCH * SEQ
CT = 512
CHUNKS = TOKENS // CT
TPC = CT // P
QK_TILES = (Q_DIM + KV_DIM) // P
Q_TILES = Q_DIM // P
TILES = TOKENS // P
VW = HD + 1
QT = SEQ // P
QC = SEQ // CT
ALL_HEADS = BATCH * HEADS
PAIRS = ALL_HEADS // 2
MASKED = -1e30
K_ROWS, M_ROW = 96, 96


class Steps:

    def __init__(self, eng, sem, base):
        self.eng, self.sem, self.at = eng, sem, base

    def do(self, ins):
        self.at = self.at + 1
        ins.then_inc(self.sem, 1)
        self.eng.wait_ge(self.sem, self.at)


def pass_waits(eng, passed):
    eng.sem_inc(passed, 1)


def part_a(nc, x_ctx, tables, tok_b, w_qkv_t, b_qk, b_v, rope, h_dram, q_hi, q_lo, k_hi, k_lo, v_dram, ident_in):
    with ExitStack() as ctx:
        sb = lambda n, s, d: ctx.enter_context(nc.sbuf_tensor(n, s, d))
        sem = lambda n: ctx.enter_context(nc.semaphore(n))
        w_hi = sb("w_hi", [P, DC, QKV_DIM], F32R)
        w_lo = sb("w_lo", [P, DC, QKV_DIM], F32R)
        x_hi = sb("x_hi", [P, DC, CT], F32R)
        x_lo = sb("x_lo", [P, DC, CT], F32R)
        hbuf = sb("hbuf", [P, TPC, D], F32)
        xn = sb("xn", [P, TPC, D], F32)
        tab = sb("tab", [P, 2, CT], F32)
        qf = sb("qf", [P, 2, CT], F32)
        qsw = sb("qsw", [P, 2, CT], F32)
        qrot = sb("qrot", [P, 2, CT], F32)
        rot_hi = sb("rot_hi", [P, 2, CT], F32R)
        rot_lo = sb("rot_lo", [P, 2, CT], F32R)
        vt = sb("vt", [P, 2, KV_HEADS, VW], F32)
        tokb = sb("tokb", [P, D], F32)
        bqk = sb("bqk", [P, QK_TILES], F32)
        bv = sb("bv", [P, KV_DIM], F32)
        ident = sb("ident", [P, P], F32)
        idx_all = sb("idx_all", [P, CHUNKS, TPC * ORDER], I32)
        idx = sb("idx", [P, TPC * ORDER], I32)
        stats = sb("stats", [P, 2, 6], F32)
        mv = sb("mv", [P, 2], F32)
        var = sb("var", [P, 1], F32)
        std = sb("std", [P, 1], F32)
        rstd = sb("rstd", [P, 1], F32)
        w_in = hbuf[:].rearrange("p t d -> p (t d)")[:, 0:2 * QKV_DIM].rearrange("p (s n) -> p s n", s=2)
        tr_ps = ctx.enter_context(nc.psum_tensor("tr_ps", [P, 2, DC, P], F32))
        qk_ps = ctx.enter_context(nc.psum_tensor("qk_ps", [P, 2, CT], F32))
        v_ps = ctx.enter_context(nc.psum_tensor("v_ps", [P, 2, 512], F32))

        consts = sem("consts")
        w_loaded = [sem(f"w_loaded{s}") for s in range(2)]
        w_hi_done, w_lo_done = sem("w_hi_done"), sem("w_lo_done")
        idx_loaded, idx_copied = sem("idx_loaded"), sem("idx_copied")
        gathered = [sem(f"gathered{t}") for t in range(TPC)]
        h_ready, h_stored = sem("h_ready"), sem("h_stored")
        ln_step, var_ready, std_ready = sem("ln_step"), sem("var_ready"), sem("std_ready")
        xn_ready, tr_ready = sem("xn_ready"), sem("tr_ready")
        x_hi_done, x_lo_done = sem("x_hi_done"), sem("x_lo_done")
        qk_ready, qf_done = sem("qk_ready"), sem("qf_done")
        rot_step, rot_done = sem("rot_step"), sem("rot_done")
        rhi_done, rlo_done = sem("rhi_done"), sem("rlo_done")
        rot_stored = [sem(f"rot_stored{s}") for s in range(2)]
        tab_loaded, ones_set = sem("tab_loaded"), sem("ones_set")
        dve_passed, pool_passed = sem("dve_passed"), sem("pool_passed")
        v_ready, v_done = sem("v_ready"), sem("v_done")
        v_stored = [sem(f"v_stored{s}") for s in range(2)]
        EMPTY = 16
        AHEAD = 2
        block = ctx.enter_context(nc.Block())

        @block.sync
        def _(sp):
            sp.dma_start(idx_all[:], x_ctx).then_inc(idx_loaded, 16)
            sp.dma_start(ident[:], ident_in).then_inc(consts, 16)
            sp.dma_start(tokb[:], tok_b.rearrange("(a d) -> a d", a=1).broadcast_to([P, D])).then_inc(consts, 16)
            sp.dma_start(bqk[:], b_qk).then_inc(consts, 16)
            sp.dma_start(bv[:], b_v.rearrange("(a d) -> a d", a=1).broadcast_to([P, KV_DIM])).then_inc(consts, 16)
            for c in range(DC):
                if c >= 2:
                    sp.wait_ge(w_lo_done, c - 1)
                sp.dma_start(w_in[:, c % 2, :], w_qkv_t[c * P:(c + 1) * P, :]).then_inc(w_loaded[c % 2], 16)
            sp.dma_start(tab[:], rope[0]).then_inc(tab_loaded, 16)

            def store_h(m):
                for t in range(TPC):
                    sp.wait_ge(h_ready, m * TPC + t + 1)
                    sp.dma_start(h_dram[bass.ds(m * CT + t * P, P), :], hbuf[:, t, :]).then_inc(h_stored, 16)

            def store_rotated(n, f):
                sp.wait_ge(rlo_done, n * QK_TILES + f + 1)
                hi, lo, row = (q_hi, q_lo, f * P) if f < Q_TILES else (k_hi, k_lo, (f - Q_TILES) * P)
                at = (slice(None), bass.ds((n % QC) * CT, CT))
                for dst, src in ((hi, rot_hi), (lo, rot_lo)):
                    dst_rows = dst[bass.ds((n // QC) * (Q_DIM if f < Q_TILES else KV_DIM) + row, P), :]
                    sp.dma_start(dst_rows[at], src[:, f % 2, :].bitcast(F32)).then_inc(rot_stored[f % 2], 16)

            def chunk(n, last):
                for f in range(QK_TILES):
                    store_rotated(n, f)
                    if not last and f == QK_TILES - 1:
                        store_h(n + 1)
                if not last:
                    sp.wait_ge(rot_done, (n + 1) * QK_TILES + AHEAD)
                    sp.dma_start(tab[:], rope[n + 1]).then_inc(tab_loaded, 16)
                for t in range(TPC):
                    sp.wait_ge(v_done, n * TPC + t + 1 + AHEAD)
                    sp.dma_start(v_dram[bass.ds(n * CT + t * P, P), :],
                                 vt[:, t % 2, :, :].rearrange("p h w -> p (h w)")).then_inc(v_stored[t % 2], 16)

            store_h(0)
            with sp.Fori(0, CHUNKS - 1) as n:
                chunk(n, False)
            chunk(CHUNKS - 1, True)
            sp.wait_ge(h_stored, 16 * TILES)
            for s in range(2):
                sp.wait_ge(rot_stored[s], EMPTY + 16 * CHUNKS * QK_TILES)
                sp.wait_ge(v_stored[s], EMPTY + 16 * CHUNKS * TPC // 2)

        @block.gpsimd
        def _(pool):
            pool.wait_ge(idx_loaded, 16)
            pool.wait_ge(w_lo_done, DC)

            def gather(m, first):
                nc.gpsimd.tensor_copy(idx[:], idx_all[:, m, :] if first else
                                      idx_all[:, bass.ds(m, 1), :].rearrange("p a k -> p (a k)")
                                      ).then_inc(idx_copied, 1)
                pool.wait_ge(idx_copied, m + 1)
                if not first:
                    pool.wait_ge(h_stored, 16 * TPC * m)
                for k in range(ORDER):
                    for t in range(TPC):
                        if k == 0 and not first:
                            pool.wait_ge(xn_ready, m * TPC - TPC + t + 1)
                        if k > 0:
                            pool.wait_ge(gathered[t], 16 * (m * ORDER + k))
                        pass_waits(pool, pool_passed)
                        j = t * ORDER + k
                        nc.gpsimd.indirect_dma_start(
                            hbuf[:, t, :], None, tables[k],
                            bass.IndirectOffsetOnAxis(ap=idx[:, j:j + 1], axis=0),
                            compute_op=ALU.bypass if k == 0 else ALU.add).then_inc(gathered[t], 16)
                for t in range(TPC):
                    pool.wait_ge(gathered[t], 16 * (m + 1) * ORDER)

            gather(0, True)
            with pool.Fori(1, CHUNKS) as m:
                gather(m, False)

        @block.scalar
        def _(act):
            act.sem_inc(qf_done, AHEAD)
            for s in range(2):
                act.sem_inc(rot_stored[s], EMPTY)
            for c in range(DC):
                act.wait_ge(w_loaded[c % 2], 16 * (c // 2 + 1))
                nc.scalar.copy(w_hi[:, c, :], w_in[:, c % 2, :]).then_inc(w_hi_done, 1)
            act.wait_ge(consts, 64)

            def deviation(m, t):
                act.wait_ge(var_ready, m * TPC + t + 1)
                nc.scalar.activation(std[:], var[:], ACT.Sqrt).then_inc(std_ready, 1)

            def x_high(m, t):
                act.wait_ge(tr_ready, m * TPC + t + 1)
                nc.scalar.copy(x_hi[:, :, t * P:(t + 1) * P], tr_ps[:, t % 2]).then_inc(x_hi_done, 1)

            def add_bias(n, f):
                act.wait_ge(qk_ready, n * QK_TILES + f + 1)
                act.wait_ge(rot_done, n * QK_TILES + f + 1)
                nc.scalar.activation(qf[:, f % 2, :], qk_ps[:, f % 2, :], ACT.Identity,
                                     bias=bqk[:, f:f + 1]).then_inc(qf_done, 1)

            def rot_high(n, f):
                act.wait_ge(rot_done, n * QK_TILES + f + 1 + AHEAD)
                act.wait_ge(rot_stored[f % 2], EMPTY + 32 * (n * (QK_TILES // 2) + f // 2))
                nc.scalar.copy(rot_hi[:, f % 2, :], qrot[:, f % 2, :]).then_inc(rhi_done, 1)

            def chunk(n, last):
                for f in range(QK_TILES):
                    add_bias(n, f)
                    if f >= 1:
                        rot_high(n, f - 1)
                    if f % 2 and f // 2 < TPC and not last:
                        deviation(n + 1, f // 2)
                rot_high(n, QK_TILES - 1)
                if not last:
                    for t in range(TPC):
                        x_high(n + 1, t)

            for t in range(TPC):
                deviation(0, t)
            for t in range(TPC):
                x_high(0, t)
            with act.Fori(0, CHUNKS - 1) as n:
                chunk(n, False)
            chunk(CHUNKS - 1, True)

        @block.vector
        def _(dve):
            dve.sem_inc(rot_done, AHEAD)
            dve.sem_inc(v_done, AHEAD)
            for s in range(2):
                dve.sem_inc(v_stored[s], EMPTY)
            nc.vector.memset(vt[:], 1.0).then_inc(ones_set, 1)
            for c in range(DC):
                dve.wait_ge(w_hi_done, c + 1)
                nc.vector.tensor_tensor(w_lo[:, c, :], w_in[:, c % 2, :], w_hi[:, c, :].bitcast(F32),
                                        ALU.subtract).then_inc(w_lo_done, 1)
            dve.wait_ge(ones_set, 1)
            dve.wait_ge(consts, 64)
            LN_STEPS, ROT_STEPS = 6, 3

            def layer_norm(m, t):
                at = m * TPC + t
                step = Steps(dve, ln_step, at * LN_STEPS)
                h = hbuf[:, t, :]
                dve.wait_ge(gathered[t], 16 * ORDER * (m + 1))
                nc.vector.tensor_tensor(h, h, tokb[:], ALU.add).then_inc(h_ready, 1)
                dve.wait_ge(h_ready, at + 1)
                step.do(nc.vector.bn_stats(stats[:, 0, :], h[:, 0:512]))
                step.do(nc.vector.bn_stats(stats[:, 1, :], h[:, 512:1024]))
                pass_waits(dve, dve_passed)
                step.do(nc.vector.bn_aggr(mv[:], stats[:].rearrange("p a s -> p (a s)")))
                nc.vector.tensor_scalar(var[:], mv[:, 1:2], EPS, None, ALU.add).then_inc(var_ready, 1)
                dve.wait_ge(std_ready, at + 1)
                step.do(nc.vector.reciprocal(rstd[:], std[:]))
                if not (isinstance(m, int) and m == 0):
                    dve.wait_ge(tr_ready, at - TPC + 1)
                nc.vector.tensor_scalar(xn[:, t, :], h, mv[:, 0:1], rstd[:], ALU.subtract,
                                        ALU.mult).then_inc(xn_ready, 1)
                dve.wait_ge(xn_ready, at + 1)
                step.do(nc.vector.tensor_copy(var[:], rstd[:]))
                step.do(nc.vector.tensor_copy(var[:], rstd[:]))

            def x_low(m, t):
                dve.wait_ge(x_hi_done, m * TPC + t + 1)
                sl = slice(t * P, (t + 1) * P)
                nc.vector.tensor_tensor(x_lo[:, :, sl], tr_ps[:, t % 2], x_hi[:, :, sl].bitcast(F32),
                                        ALU.subtract).then_inc(x_lo_done, 1)

            swap = [i ^ 1 for i in range(32)]

            def rotate(n, f):
                at = n * QK_TILES + f
                step = Steps(dve, rot_step, at * ROT_STEPS)
                s = f % 2
                dve.wait_ge(qf_done, at + 1 + AHEAD)
                if f == 0:
                    dve.wait_ge(tab_loaded, 16 * (n + 1))
                pass_waits(dve, dve_passed)
                step.do(nc.vector.stream_shuffle(qsw[:, s, :], qf[:, s, :], swap))
                step.do(nc.vector.tensor_tensor(qsw[:, s, :], qsw[:, s, :], tab[:, 1, :], ALU.mult))
                step.do(nc.vector.tensor_tensor(qrot[:, s, :], qf[:, s, :], tab[:, 0, :], ALU.mult))
                nc.vector.tensor_tensor(qrot[:, s, :], qrot[:, s, :], qsw[:, s, :], ALU.add).then_inc(rot_done, 1)

            def rot_low(n, f):
                dve.wait_ge(rhi_done, n * QK_TILES + f + 1)
                nc.vector.tensor_tensor(rot_lo[:, f % 2, :], qrot[:, f % 2, :], rot_hi[:, f % 2, :].bitcast(F32),
                                        ALU.subtract).then_inc(rlo_done, 1)

            def values(n, t):
                dve.wait_ge(v_ready, n * TPC + t + 1)
                dve.wait_ge(v_stored[t % 2], EMPTY + 16 * (n * (TPC // 2) + t // 2))
                nc.vector.tensor_tensor(vt[:, t % 2, :, 0:HD],
                                        v_ps[:, t % 2, 0:KV_DIM].rearrange("p (h w) -> p h w", w=HD),
                                        bv[:].rearrange("p (h w) -> p h w", w=HD), ALU.add).then_inc(v_done, 1)

            def chunk(n, last):
                for f in range(QK_TILES):
                    rotate(n, f)
                    if f >= 1:
                        rot_low(n, f - 1)
                    if f % 2 and f // 2 < TPC and not last:
                        layer_norm(n + 1, f // 2)
                rot_low(n, QK_TILES - 1)
                for t in range(TPC):
                    values(n, t)
                    if not last:
                        x_low(n + 1, t)

            for t in range(TPC):
                layer_norm(0, t)
            for t in range(TPC):
                x_low(0, t)
            with dve.Fori(0, CHUNKS - 1) as n:
                chunk(n, False)
            chunk(CHUNKS - 1, True)

        @block.tensor
        def _(pe):
            pe.wait_ge(consts, 64)
            pe.wait_ge(w_lo_done, DC)

            def transpose(m, t):
                at = m * TPC + t
                pe.wait_ge(xn_ready, at + 1)
                if not (isinstance(m, int) and m == 0 and t < 2):
                    pe.wait_ge(x_lo_done, at - 1)
                for c in range(DC):
                    mm = nc.tensor.transpose(tr_ps[:, t % 2, c, :], xn[:, t, c * P:(c + 1) * P], ident[:])
                mm.then_inc(tr_ready, 1)

            def chunk(n, last):
                pe.wait_ge(x_lo_done, (n + 1) * TPC)
                for f in range(QK_TILES):
                    pe.wait_ge(qf_done, n * QK_TILES + f + 1)
                    for c in range(DC):
                        w = (w_hi[:, c, f * P:(f + 1) * P], w_lo[:, c, f * P:(f + 1) * P])
                        x = (x_hi[:, c, :], x_lo[:, c, :])
                        for k, (a, b) in enumerate(((0, 0), (0, 1), (1, 0))):
                            mm = nc.tensor.matmul(qk_ps[:, f % 2, :], w[a], x[b], start=(c == 0 and k == 0),
                                                  stop=(c == DC - 1 and k == 2))
                    mm.then_inc(qk_ready, 1)
                for t in range(TPC):
                    pe.wait_ge(v_done, n * TPC + t + 1)
                    for c in range(DC):
                        w = (w_hi[:, c, Q_DIM + KV_DIM:], w_lo[:, c, Q_DIM + KV_DIM:])
                        x = (x_hi[:, c, t * P:(t + 1) * P], x_lo[:, c, t * P:(t + 1) * P])
                        for k, (a, b) in enumerate(((0, 0), (1, 0), (0, 1))):
                            mm = nc.tensor.matmul(v_ps[:, t % 2, 0:KV_DIM], x[b], w[a], start=(c == 0 and k == 0),
                                                  stop=(c == DC - 1 and k == 2))
                    mm.then_inc(v_ready, 1)
                    if not last:
                        transpose(n + 1, t)

            for t in range(TPC):
                transpose(0, t)
            with pe.Fori(0, CHUNKS - 1) as n:
                chunk(n, False)
            chunk(CHUNKS - 1, True)


def score_units():
    return [(c, kt, max(0, kt - c * TPC)) for c in range(QC) for kt in range(TPC * (c + 1))]


def max_units():
    return [(i, j, CT if j < i // TPC else (i % TPC + 1) * P) for i in range(QT) for j in range(i // TPC + 1)]


UNITS, MAXES = score_units(), max_units()
NU, NM = len(UNITS), len(MAXES)
LAST_OF = [max(u for u, (c, _, _) in enumerate(UNITS) if c == k) for k in range(QC)]
LAG = 2
TURN = 34


def head_plan(next_head):
    plan, n = [], 0
    for u in range(NU + LAG):
        if u < NU:
            plan.append(("score", u))
        while next_head and n < min(NM, (u + 1) * 5 // 4):
            plan.append(("max", n))
            n += 1
            if n == NM:
                plan.append(("max_all", 0))
        if u >= LAG:
            plan.append(("value", u - LAG))
        if next_head and u == TURN:
            plan.append(("turn", 0))
    return plan


def part_b(nc, q_hi, q_lo, k_hi, k_lo, v_dram, ao_dram, ident_in, mask_qk, mask_kq):
    with ExitStack() as ctx:
        sb = lambda n, s, d: ctx.enter_context(nc.sbuf_tensor(n, s, d))
        sem = lambda n: ctx.enter_context(nc.semaphore(n))
        qs = [sb(f"qs{s}", [P, SEQ], F32R) for s in range(2)]
        ks = [sb(f"ks{s}", [P, SEQ], F32R) for s in range(2)]
        v_all = sb("v_all", [P, TILES, KV_HEADS, VW], F32)
        v_cur = sb("v_cur", [P, 2, QT, VW], F32)
        probs = sb("probs", [P, 4, CT], F32)
        ao = sb("ao", [P, QT, 2, HD], F32)
        recip = sb("recip", [P, TPC], F32)
        mpart = sb("mpart", [P, QT, QC], F32)
        mrow = sb("mrow", [P, QT], F32)
        m_hi = sb("m_hi", [QT, P], F32R)
        m_lo = sb("m_lo", [QT, P], F32R)
        ident = sb("ident_b", [P, P], F32)
        consts_in = sb("consts_in", [P, 3, P], F32)
        consts_r = sb("consts_r", [P, 3, P], F32R)
        identr, mqk, mkq = (consts_r[:, j, :] for j in range(3))
        st_ps = ctx.enter_context(nc.psum_tensor("st_ps", [P, 3, CT], F32))
        mx_ps = ctx.enter_context(nc.psum_tensor("mx_ps", [P, 2, CT], F32))
        o_ps = ctx.enter_context(nc.psum_tensor("o_ps", [P, 2, 512], F32))
        mt_ps = ctx.enter_context(nc.psum_tensor("mt_ps", [P, 512], F32))

        loaded = [sem(f"loaded{s}") for s in range(2)]
        consts, consts_done, ones_done = sem("consts_b"), sem("consts_done"), sem("ones_done")
        v_loaded, v_copied = sem("v_loaded"), sem("v_copied")
        max_ready, max_done, max_all = sem("max_ready"), sem("max_done"), sem("max_all")
        turned, m_hi_done, m_lo_done, m_rows = sem("turned"), sem("m_hi_done"), sem("m_lo_done"), sem("m_rows")
        st_ready, exp_done, pv_done = sem("st_ready"), sem("exp_done"), sem("pv_done")
        recip_done, o_done = sem("recip_done"), sem("o_done")
        ao_stored = [sem(f"ao_stored{c}") for c in range(QC)]
        P_FREE, O_FREE = 4, 2
        EMPTY = 16
        LOADS = 6 * 16
        block = ctx.enter_context(nc.Block())

        def slots(i, last):
            return ((i * 2, 0, True), (i * 2 + 1, 1, not last))

        @block.sync
        def _(sp):
            for j, a in enumerate((ident_in, mask_qk, mask_kq)):
                sp.dma_start(consts_in[:, j, :], a).then_inc(consts, 16)
            sp.dma_start(ident[:], ident_in).then_inc(consts, 16)

            def load(h, s):
                q_row = (h // HEADS) * Q_DIM + (h % HEADS) * HD
                k_row = (h // GROUP) * HD
                for r, (q, k) in enumerate(((q_hi, k_hi), (q_hi, k_lo), (q_lo, k_hi))):
                    rows = slice(r * HD, (r + 1) * HD)
                    sp.dma_start(qs[s][rows, :].bitcast(F32), q[bass.ds(q_row, HD), :]).then_inc(loaded[s], 16)
                    sp.dma_start(ks[s][rows, :].bitcast(F32), k[bass.ds(k_row, HD), :]).then_inc(loaded[s], 16)

            def store(i):
                for c in range(QC):
                    sp.wait_ge(o_done, O_FREE + (2 * i + 1) * QC + c + 1)
                    rows = ao_dram[bass.ds(i * SEQ + c * CT, CT), :].rearrange("(t p) n -> p t n", p=P)
                    sp.dma_start(rows, ao[:, c * TPC:(c + 1) * TPC].rearrange("p t s n -> p t (s n)")
                                 ).then_inc(ao_stored[c], 16)

            load(0, 0)
            load(1, 1)
            sp.dma_start(v_all[:].rearrange("p t h w -> p t (h w)"),
                         v_dram.rearrange("(t p) n -> p t n", p=P)).then_inc(v_loaded, 16)
            with sp.Fori(0, PAIRS - 1) as i:
                sp.wait_ge(pv_done, P_FREE + (2 * i + 1) * NU)
                load(2 * i + 2, 0)
                store(i)
                sp.wait_ge(pv_done, P_FREE + (2 * i + 2) * NU)
                load(2 * i + 3, 1)
            store(PAIRS - 1)
            for c in range(QC):
                sp.wait_ge(ao_stored[c], EMPTY + 16 * PAIRS)

        @block.gpsimd
        def _(pool):
            pool.wait_ge(consts, 64)
            nc.gpsimd.tensor_copy(consts_r[:], consts_in[:]).then_inc(consts_done, 1)
            pool.wait_ge(v_loaded, 16)

            def copy_v(i):
                for h, s, _ in slots(i, False):
                    if not isinstance(h, int):
                        pool.wait_ge(pv_done, P_FREE + (h - 1) * NU)
                    src = v_all[:, bass.ds((h // HEADS) * QT, QT), bass.ds((h // GROUP) % KV_HEADS, 1), :]
                    nc.gpsimd.tensor_copy(v_cur[:, s], src.rearrange("p t a w -> p t (a w)")).then_inc(v_copied, 1)

            copy_v(0)
            with pool.Fori(1, PAIRS) as i:
                copy_v(i)

        @block.scalar
        def _(act):
            def head(h, s, more):
                for what, u in head_plan(more):
                    if what == "score":
                        c, kt, j = UNITS[u]
                        w = CT - j * P
                        act.wait_ge(st_ready, h * NU + u + 1)
                        act.wait_ge(pv_done, h * NU + u + 1)
                        nc.scalar.activation(probs[:, u % 4, 0:w], st_ps[:, u % 3, 0:w], ACT.Exp,
                                             scale=float(HD) ** -0.5).then_inc(exp_done, 1)
                    if what == "turn":
                        turn(h + 1, 1 - s)

            def turn(h, s):
                act.wait_ge(turned, h + 1)
                if not (isinstance(h, int) and h == 0):
                    act.wait_ge(m_rows, 32 * h)
                nc.scalar.mul(m_hi[:], mt_ps[0:QT, 0:P], -1.0).then_inc(m_hi_done, 1)
                act.wait_ge(m_hi_done, h + 1)
                act.dma_start(qs[s][M_ROW:M_ROW + 1, :].bitcast(F32).rearrange("a (t p) -> a t p", p=P), m_hi[:].bitcast(F32)
                              ).then_inc(m_rows, 16)
                act.wait_ge(m_lo_done, h + 1)
                act.dma_start(qs[s][M_ROW + 1:M_ROW + 2, :].bitcast(F32).rearrange("a (t p) -> a t p", p=P), m_lo[:].bitcast(F32)
                              ).then_inc(m_rows, 16)

            turn(0, 0)
            with act.Fori(0, PAIRS - 1) as i:
                for h, s, more in slots(i, False):
                    head(h, s, more)
            for h, s, more in slots(PAIRS - 1, True):
                head(h, s, more)

        @block.vector
        def _(dve):
            dve.sem_inc(pv_done, P_FREE)
            dve.sem_inc(o_done, O_FREE)
            for c in range(QC):
                dve.sem_inc(ao_stored[c], EMPTY)
            for s in range(2):
                nc.vector.memset(ks[s][M_ROW:P, :].bitcast(F32), 1.0).then_inc(ones_done, 1)

            def row_max(h, n):
                i, j, w = MAXES[n]
                dve.wait_ge(max_ready, h * NM + n + 1)
                if n == 0 and not (isinstance(h, int) and h == 0):
                    dve.wait_ge(max_all, h)
                nc.vector.tensor_reduce(mpart[:, i, j:j + 1], mx_ps[:, n % 2, 0:w], AX, ALU.max
                                        ).then_inc(max_done, 1)

            def all_max(h):
                dve.wait_ge(max_done, (h + 1) * NM)
                for g in range(QC):
                    last = nc.vector.tensor_reduce(mrow[:, g * TPC:(g + 1) * TPC],
                                                   mpart[:, g * TPC:(g + 1) * TPC, 0:g + 1], AX, ALU.max)
                last.then_inc(max_all, 1)

            def turn_low(h):
                dve.wait_ge(m_hi_done, h + 1)
                nc.vector.scalar_tensor_tensor(m_lo[:], mt_ps[0:QT, 0:P], -1.0, m_hi[:].bitcast(F32),
                                               ALU.mult, ALU.subtract).then_inc(m_lo_done, 1)

            def normalise(h, s, c, pair):
                dve.wait_ge(pv_done, P_FREE + h * NU + LAST_OF[c] + 1)
                o = o_ps[:, c % 2, 0:TPC * VW].rearrange("p (t w) -> p t w", w=VW)
                if not (isinstance(h, int) and h == 0):
                    dve.wait_ge(o_done, O_FREE + h * QC + c)
                elif c:
                    dve.wait_ge(o_done, O_FREE + c)
                nc.vector.reciprocal(recip[:], o[:, :, HD]).then_inc(recip_done, 1)
                dve.wait_ge(recip_done, h * QC + c + 1)
                if s == 0:
                    dve.wait_ge(ao_stored[c], EMPTY + 16 * pair)
                nc.vector.tensor_tensor(ao[:, c * TPC:(c + 1) * TPC, s, :], o[:, :, 0:HD],
                                        recip[:].rearrange("p (t a) -> p t a", a=1).broadcast_to([P, TPC, HD]),
                                        ALU.mult).then_inc(o_done, 1)

            def head(h, s, more, pair):
                for what, u in head_plan(more):
                    if what == "max":
                        row_max(h + 1, u)
                    if what == "max_all":
                        all_max(h + 1)
                    if what == "turn":
                        turn_low(h + 1)
                    if what == "value" and u in LAST_OF:
                        normalise(h, s, LAST_OF.index(u), pair)

            for n in range(NM):
                row_max(0, n)
            all_max(0)
            turn_low(0)
            with dve.Fori(0, PAIRS - 1) as i:
                for h, s, more in slots(i, False):
                    head(h, s, more, i)
            for h, s, more in slots(PAIRS - 1, True):
                head(h, s, more, PAIRS - 1)

        @block.tensor
        def _(pe):
            pe.wait_ge(consts_done, 1)
            pe.wait_ge(ones_done, 2)

            def row_scores(h, s, n, seen):
                i, j, w = MAXES[n]
                if n == 0:
                    pe.wait_ge(loaded[s], LOADS * seen)
                if not (isinstance(h, int) and h == 0 and n < 2):
                    pe.wait_ge(max_done, h * NM + n - 1)
                diagonal = j == i // TPC
                out = mx_ps[:, n % 2, 0:w]
                mm = nc.tensor.matmul(out, qs[s][0:K_ROWS, i * P:(i + 1) * P], ks[s][0:K_ROWS, j * CT:j * CT + w],
                                      start=True, stop=not diagonal)
                if diagonal:
                    mm = nc.tensor.matmul(out[:, w - P:w], identr, mqk, start=False, stop=True)
                mm.then_inc(max_ready, 1)

            def turn(h):
                pe.wait_ge(max_all, h + 1)
                if not (isinstance(h, int) and h == 0):
                    pe.wait_ge(m_lo_done, h)
                nc.tensor.transpose(mt_ps[0:QT, 0:P], mrow[:], ident[:]).then_inc(turned, 1)

            def scores(h, s, u):
                c, kt, j = UNITS[u]
                w = CT - j * P
                if u == 0:
                    pe.wait_ge(m_rows, 32 * (h + 1))
                if u >= 3:
                    pe.wait_ge(exp_done, h * NU + u - 2)
                diagonal = kt >= c * TPC
                mm = nc.tensor.matmul(st_ps[:, u % 3, 0:w], ks[s][0:M_ROW + 2, kt * P:(kt + 1) * P],
                                      qs[s][0:M_ROW + 2, c * CT + j * P:(c + 1) * CT], start=True, stop=not diagonal)
                if diagonal:
                    mm = nc.tensor.matmul(st_ps[:, u % 3, 0:P], identr, mkq, start=False, stop=True)
                mm.then_inc(st_ready, 1)

            def values(h, s, u):
                c, kt, j = UNITS[u]
                pe.wait_ge(exp_done, h * NU + u + 1)
                if u == 0:
                    pe.wait_ge(v_copied, h + 1)
                if kt == 0:
                    pe.wait_ge(o_done, h * QC + c + 1)
                for t in range(j, TPC):
                    mm = nc.tensor.matmul(o_ps[:, c % 2, t * VW:(t + 1) * VW],
                                          probs[:, u % 4, (t - j) * P:(t - j + 1) * P], v_cur[:, s, kt, :],
                                          start=(kt == 0 and t == 0), stop=(kt == c * TPC + t), skip_group_check=True)
                mm.then_inc(pv_done, 1)

            def head(h, s, more, seen):
                for what, u in head_plan(more):
                    if what == "score":
                        scores(h, s, u)
                    if what == "value":
                        values(h, s, u)
                    if what == "max":
                        row_scores(h + 1, 1 - s, u, seen)
                    if what == "turn":
                        turn(h + 1)

            for n in range(NM):
                row_scores(0, 0, n, 1)
            turn(0)
            with pe.Fori(0, PAIRS - 1) as i:
                for h, s, more in slots(i, False):
                    head(h, s, more, i + 1 + s)
            for h, s, more in slots(PAIRS - 1, True):
                head(h, s, more, PAIRS + s)


def part_c(nc, ao_dram, h_dram, w_o_t, b_o, w_base_t, b_base, enc, coefs, mask, fourier_t, ident_in, out):
    with ExitStack() as ctx:
        sb = lambda n, s, d: ctx.enter_context(nc.sbuf_tensor(n, s, d))
        sem = lambda n: ctx.enter_context(nc.semaphore(n))
        w_hi = sb("wc_hi", [P, 2, DC, D], F32R)
        w_lo = sb("wc_lo", [P, 2, DC, D], F32R)
        a_in = sb("a_in", [P, 2, D], F32)
        h_in = sb("h_in", [P, 2, D], F32)
        h1 = sb("h1", [P, 2, D], F32)
        h1b = sb("h1b", [P, 2, D], F32)
        xn = sb("xn_c", [P, D], F32)
        a_hi, a_lo = sb("a_hi", [P, DC, P], F32R), sb("a_lo", [P, DC, P], F32R)
        x_hi, x_lo = sb("xc_hi", [P, DC, P], F32R), sb("xc_lo", [P, DC, P], F32R)
        bo, bb = sb("bo", [P, D], F32), sb("bb", [P, D], F32)
        ident = sb("ident_c", [P, P], F32)
        stats, mv = sb("stats_c", [P, 2, 6], F32), sb("mv_c", [P, 2], F32)
        var, std, rstd = sb("var_c", [P, 1], F32), sb("std_c", [P, 1], F32), sb("rstd_c", [P, 1], F32)
        enc_sb = sb("enc_sb", [R, D], F32)
        cf = h1[:].rearrange("p a d -> p (a d)")[:, 0:DC * E * R].rearrange("p (c e r) -> p c e r", e=E, r=R)
        mk8 = sb("mk8", [P, DC, E, R], U8)
        mkf = h1b[:].rearrange("p a d -> p (a d)")[:, 0:DC * E * R].rearrange("p (c e r) -> p c e r", e=E, r=R)
        wr = xn[:, 0:DC * R].rearrange("p (c r) -> p c r", r=R)
        tw = sb("tw", [R, D], F32)
        t1_ps = ctx.enter_context(nc.psum_tensor("t1_ps", [P, DC, P], F32))
        t2_ps = ctx.enter_context(nc.psum_tensor("t2_ps", [P, DC, P], F32))
        o_ps = ctx.enter_context(nc.psum_tensor("oc_ps", [P, D], F32))
        f_ps = ctx.enter_context(nc.psum_tensor("f_ps", [P, D], F32))

        consts, coefs_in, four_in = sem("consts_c"), sem("coefs_in"), [sem(f"four_in{s}") for s in range(2)]
        w_in_sem = [sem(f"w_in{s}") for s in range(2)]
        prep, tw_ps_done, tw_done = sem("prep"), sem("tw_ps_done"), sem("tw_done")
        delta_ready, wsum_done = sem("delta_ready"), sem("wsum_done")
        w_hi_done, w_lo_done = sem("wc_hi_done"), sem("wc_lo_done")
        a_loaded = [sem(f"a_loaded{s}") for s in range(2)]
        h_loaded = [sem(f"h_loaded{s}") for s in range(2)]
        hb_done, t1_ready, a_hi_done, a_lo_done = sem("hb_done"), sem("t1_ready"), sem("a_hi_done"), sem("a_lo_done")
        o_ready, h1_done, h1b_done = sem("o_ready"), sem("h1_done"), sem("h1b_done")
        ln_step, var_ready, std_ready, xn_ready = sem("ln_step_c"), sem("var_ready_c"), sem("std_ready_c"), sem("xn_ready_c")
        t2_ready, x_hi_done, x_lo_done, f_ready = sem("t2_ready"), sem("xc_hi_done"), sem("xc_lo_done"), sem("f_ready")
        out_done, dve_passed = sem("out_done"), sem("dve_passed_c")
        out_stored = [sem(f"out_stored{s}") for s in range(2)]
        EMPTY = 16
        NW = 2 * DC
        block = ctx.enter_context(nc.Block())

        @block.sync
        def _(sp):
            for c in range(DC):
                sp.dma_start(cf[:, c], coefs[:, c * P:(c + 1) * P, :].rearrange("e p r -> p e r")).then_inc(coefs_in, 16)
                sp.dma_start(mk8[:, c], mask[:, c * P:(c + 1) * P, :].rearrange("e p r -> p e r")).then_inc(coefs_in, 16)
            sp.dma_start(enc_sb[:], enc).then_inc(consts, 16)
            sp.dma_start(ident[:], ident_in).then_inc(consts, 16)
            for dst, b in ((bo, b_o), (bb, b_base)):
                sp.dma_start(dst[:], b.rearrange("(a d) -> a d", a=1).broadcast_to([P, D])).then_inc(consts, 16)
            for c in range(DC):
                if c >= 2:
                    sp.wait_ge(tw_ps_done, c - 1)
                sp.dma_start(h_in[:, c % 2, :], fourier_t[c * P:(c + 1) * P, :]).then_inc(four_in[c % 2], 16)
                if c >= 2:
                    sp.wait_ge(w_lo_done, c - 1)
                sp.dma_start(a_in[:, c % 2, :], w_o_t[c * P:(c + 1) * P, :]).then_inc(w_in_sem[c % 2], 16)
            for c in range(DC):
                sp.wait_ge(w_lo_done, DC + c - 1)
                sp.dma_start(a_in[:, c % 2, :], w_base_t[c * P:(c + 1) * P, :]).then_inc(w_in_sem[c % 2], 16)

            def load(t, s):
                rows = ao_dram[bass.ds((t // QT) * (HEADS // 2) * SEQ, (HEADS // 2) * SEQ), :]
                rows = rows.rearrange("(g q) n -> q g n", q=SEQ)[bass.ds((t % QT) * P, P), :, :]
                sp.dma_start(a_in[:, s, :].rearrange("p (g n) -> p g n", n=2 * HD), rows).then_inc(a_loaded[s], 16)
                sp.dma_start(h_in[:, s, :], h_dram[bass.ds(t * P, P), :]).then_inc(h_loaded[s], 16)

            def store(t, s):
                sp.wait_ge(out_done, t + 1)
                sp.dma_start(out[bass.ds(t * P, P), :], h1[:, s, :]).then_inc(out_stored[s], 16)

            sp.wait_ge(w_lo_done, NW)
            sp.wait_ge(tw_ps_done, DC)
            load(0, 0)
            load(1, 1)

            def tile(t, s, more):
                if more:
                    sp.wait_ge(t1_ready, t + 1)
                    sp.wait_ge(h1_done, t + 1)
                    load(t + 2, s)
                store(t, s)

            with sp.Fori(0, TILES // 2 - 1) as i:
                for s in range(2):
                    tile(2 * i + s, s, True)
            for s in range(2):
                tile(TILES - 2 + s, s, False)
            for s in range(2):
                sp.wait_ge(out_stored[s], EMPTY + 16 * TILES // 2)

        @block.gpsimd
        def _(pool):
            pool.wait_ge(consts, 64)

            def residual(t, s):
                pool.wait_ge(h_loaded[s], 16 * ((t - s) // 2 + 1) if isinstance(t, int) else 8 * (t - s) + 16)
                nc.gpsimd.tensor_tensor(h_in[:, s, :], h_in[:, s, :], bo[:], ALU.add).then_inc(hb_done, 1)
                pool.wait_ge(h1_done, t + 1)
                nc.gpsimd.tensor_tensor(h1b[:, s, :], h1[:, s, :], bb[:], ALU.add).then_inc(h1b_done, 1)

            pool.wait_ge(w_lo_done, NW)
            with pool.Fori(0, TILES // 2) as i:
                for s in range(2):
                    residual(2 * i + s, s)

        @block.scalar
        def _(act):
            for c in range(NW):
                l, k = c // DC, c % DC
                if l == 0:
                    act.wait_ge(w_in_sem[c % 2], 16 * (c // 2 + 1))
                else:
                    act.wait_ge(wsum_done, k + 1)
                nc.scalar.copy(w_hi[:, l, k, :], a_in[:, c % 2, :]).then_inc(w_hi_done, 1)

            def a_high(t):
                act.wait_ge(t1_ready, t + 1)
                if not (isinstance(t, int) and t == 0):
                    act.wait_ge(o_ready, t)
                nc.scalar.copy(a_hi[:], t1_ps[:]).then_inc(a_hi_done, 1)

            def tile(t, more):
                if more:
                    a_high(t + 1)
                act.wait_ge(var_ready, t + 1)
                nc.scalar.activation(std[:], var[:], ACT.Sqrt).then_inc(std_ready, 1)
                act.wait_ge(t2_ready, t + 1)
                nc.scalar.copy(x_hi[:], t2_ps[:]).then_inc(x_hi_done, 1)

            a_high(0)
            with act.Fori(0, TILES - 1) as t:
                tile(t, True)
            tile(TILES - 1, False)

        @block.vector
        def _(dve):
            for s in range(2):
                dve.sem_inc(out_stored[s], EMPTY)
            dve.wait_ge(coefs_in, 16 * 2 * DC)
            step = Steps(dve, prep, 0)
            step.do(nc.vector.tensor_copy(mkf, mk8[:]))
            step.do(nc.vector.tensor_tensor(cf, cf, mkf, ALU.mult))
            step.do(nc.vector.tensor_tensor(wr, cf[:, :, 0, :], cf[:, :, 1, :], ALU.add))
            step.do(nc.vector.tensor_tensor(wr, wr, cf[:, :, 2, :], ALU.add))

            def w_low(c):
                dve.wait_ge(w_hi_done, c + 1)
                nc.vector.tensor_tensor(w_lo[:, c // DC, c % DC, :], a_in[:, c % 2, :],
                                        w_hi[:, c // DC, c % DC, :].bitcast(F32), ALU.subtract).then_inc(w_lo_done, 1)

            for c in range(DC):
                w_low(c)
            dve.wait_ge(tw_ps_done, DC)
            nc.vector.tensor_scalar(tw[:], o_ps[0:R, :], SCALING, None, ALU.mult).then_inc(tw_done, 1)
            for c in range(DC):
                dve.wait_ge(w_in_sem[c % 2], 16 * ((DC + c) // 2 + 1))
                dve.wait_ge(delta_ready, c + 1)
                nc.vector.tensor_tensor(a_in[:, c % 2, :], a_in[:, c % 2, :], f_ps[:], ALU.add).then_inc(wsum_done, 1)
                dve.wait_ge(wsum_done, c + 1)
                w_low(DC + c)
            LN_STEPS = 4

            def a_low(t):
                dve.wait_ge(a_hi_done, t + 1)
                nc.vector.tensor_tensor(a_lo[:], t1_ps[:], a_hi[:].bitcast(F32), ALU.subtract).then_inc(a_lo_done, 1)

            def finish(t, s):
                dve.wait_ge(f_ready, t + 1)
                dve.wait_ge(h1b_done, t + 1)
                nc.vector.tensor_tensor(h1[:, s, :], f_ps[:], h1b[:, s, :], ALU.add).then_inc(out_done, 1)

            def tile(t, s, more, first):
                if more:
                    a_low(t + 1)
                dve.wait_ge(o_ready, t + 1)
                dve.wait_ge(hb_done, t + 1)
                stored = 16 * (t // 2) if isinstance(t, int) else 8 * (t - s)
                dve.wait_ge(out_stored[s], EMPTY + stored)
                nc.vector.tensor_tensor(h1[:, s, :], o_ps[:], h_in[:, s, :], ALU.add).then_inc(h1_done, 1)
                dve.wait_ge(h1_done, t + 1)
                st = Steps(dve, ln_step, t * LN_STEPS)
                st.do(nc.vector.bn_stats(stats[:, 0, :], h1[:, s, 0:512]))
                st.do(nc.vector.bn_stats(stats[:, 1, :], h1[:, s, 512:1024]))
                pass_waits(dve, dve_passed)
                st.do(nc.vector.bn_aggr(mv[:], stats[:].rearrange("p a s -> p (a s)")))
                nc.vector.tensor_scalar(var[:], mv[:, 1:2], EPS, None, ALU.add).then_inc(var_ready, 1)
                dve.wait_ge(std_ready, t + 1)
                st.do(nc.vector.reciprocal(rstd[:], std[:]))
                if not first:
                    dve.wait_ge(t2_ready, t)
                nc.vector.tensor_scalar(xn[:], h1[:, s, :], mv[:, 0:1], rstd[:], ALU.subtract,
                                        ALU.mult).then_inc(xn_ready, 1)
                dve.wait_ge(xn_ready, t + 1)
                if not first:
                    finish(t - 1, 1 - s)
                dve.wait_ge(x_hi_done, t + 1)
                nc.vector.tensor_tensor(x_lo[:], t2_ps[:], x_hi[:].bitcast(F32), ALU.subtract).then_inc(x_lo_done, 1)

            a_low(0)
            tile(0, 0, True, True)
            with dve.Fori(0, TILES // 2 - 1) as i:
                for s in (1, 0):
                    tile(2 * i + 2 - s, s, True, False)
            tile(TILES - 1, 1, False, False)
            finish(TILES - 1, 1)

        @block.tensor
        def _(pe):
            pe.wait_ge(prep, 4)
            for c in range(DC):
                pe.wait_ge(four_in[c % 2], 16 * (c // 2 + 1))
                for n in range(2):
                    mm = nc.tensor.matmul(o_ps[0:R, n * 512:(n + 1) * 512], wr[:, c, :],
                                          h_in[:, c % 2, n * 512:(n + 1) * 512], start=(c == 0), stop=(c == DC - 1))
                mm.then_inc(tw_ps_done, 1)
            pe.wait_ge(tw_done, 1)
            pe.wait_ge(consts, 64)
            for c in range(DC):
                if c:
                    pe.wait_ge(wsum_done, c)
                for n in range(2):
                    mm = nc.tensor.matmul(f_ps[:, n * 512:(n + 1) * 512], enc_sb[:, c * P:(c + 1) * P],
                                          tw[:, n * 512:(n + 1) * 512], start=True, stop=True)
                mm.then_inc(delta_ready, 1)
            pe.wait_ge(w_lo_done, NW)

            def turn_a(t, s):
                pe.wait_ge(a_loaded[s], 16 * (t // 2 + 1) if isinstance(t, int) else 8 * (t - s) + 16)
                if not (isinstance(t, int) and t == 0):
                    pe.wait_ge(a_lo_done, t)
                for c in range(DC):
                    mm = nc.tensor.transpose(t1_ps[:, c, :], a_in[:, s, c * P:(c + 1) * P], ident[:])
                mm.then_inc(t1_ready, 1)

            def turn_x(t):
                pe.wait_ge(xn_ready, t + 1)
                if not (isinstance(t, int) and t == 0):
                    pe.wait_ge(x_lo_done, t)
                for c in range(DC):
                    mm = nc.tensor.transpose(t2_ps[:, c, :], xn[:, c * P:(c + 1) * P], ident[:])
                mm.then_inc(t2_ready, 1)

            def product(out_ps, x, l, done):
                for c in range(DC):
                    for k, (a, b) in enumerate(((0, 0), (0, 1), (1, 0))):
                        for n in range(2):
                            mm = nc.tensor.matmul(out_ps[:, n * 512:(n + 1) * 512], x[a][:, c, :],
                                                  (w_hi, w_lo)[b][:, l, c, n * 512:(n + 1) * 512],
                                                  start=(c == 0 and k == 0), stop=(c == DC - 1 and k == 2))
                mm.then_inc(done, 1)

            def project(t):
                pe.wait_ge(a_lo_done, t + 1)
                if not (isinstance(t, int) and t == 0):
                    pe.wait_ge(h1_done, t)
                product(o_ps, (a_hi, a_lo), 0, o_ready)

            def last_layer(t):
                pe.wait_ge(x_lo_done, t + 1)
                if not (isinstance(t, int) and t == 0):
                    pe.wait_ge(out_done, t)
                product(f_ps, (x_hi, x_lo), 1, f_ready)

            turn_a(0, 0)
            project(0)
            turn_a(1, 1)
            turn_x(0)
            with pe.Fori(0, TILES // 2 - 1) as i:
                for s in (1, 0):
                    t = 2 * i + 2 - s
                    project(t)
                    turn_a(t + 1, 1 - s)
                    last_layer(t - 1)
                    turn_x(t)
            project(TILES - 1)
            last_layer(TILES - 2)
            turn_x(TILES - 1)
            last_layer(TILES - 1)


def build(nc, x_ctx, t0, t1, t2, t3, tok_b, w_qkv_t, b_qk, b_v, w_o_t, b_o, w_base_t, b_base, enc, coefs, mask,
          rope, fourier_t, ident, mask_qk, mask_kq, out):
    scratch = lambda n, s, d: nc.dram_tensor(n, s, d, kind="Internal").ap()
    h_dram = scratch("h_scratch", [TOKENS, D], F32)
    q_hi = scratch("q_hi_scratch", [BATCH * Q_DIM, SEQ], F32)
    q_lo = scratch("q_lo_scratch", [BATCH * Q_DIM, SEQ], F32)
    k_hi = scratch("k_hi_scratch", [BATCH * KV_DIM, SEQ], F32)
    k_lo = scratch("k_lo_scratch", [BATCH * KV_DIM, SEQ], F32)
    v_dram = scratch("v_scratch", [TOKENS, KV_HEADS * VW], F32)
    ao_dram = scratch("ao_scratch", [PAIRS * SEQ, 2 * HD], F32)
    part_a(nc, x_ctx, (t0, t1, t2, t3), tok_b, w_qkv_t, b_qk, b_v, rope, h_dram, q_hi, q_lo, k_hi, k_lo, v_dram, ident)
    part_b(nc, q_hi, q_lo, k_hi, k_lo, v_dram, ao_dram, ident, mask_qk, mask_kq)
    part_c(nc, ao_dram, h_dram, w_o_t, b_o, w_base_t, b_base, enc, coefs, mask, fourier_t, ident, out)


def rope_table():
    inv = (1.0 / np.float32(10000.0) ** (np.arange(0, HD, 2, dtype=np.float32) / np.float32(HD))).astype(np.float32)
    ang = np.arange(SEQ, dtype=np.float32)[:, None] * inv[None, :]
    cos, sin = np.cos(ang).T, np.sin(ang).T
    cos = np.repeat(cos, 2, axis=0)
    sin = np.stack([-sin, sin], axis=1).reshape(HD, SEQ)
    tab = np.tile(np.stack([cos, sin], axis=1), (P // HD, 1, 1))
    tab = tab.reshape(P, 2, QC, CT).transpose(2, 0, 1, 3)
    return np.ascontiguousarray(np.concatenate([tab] * BATCH)).astype(np.float32)


def fourier_matrix_t():
    n = D
    o = np.arange(n)
    rows = np.zeros((n, n))
    rows[0] = 1.0 / np.sqrt(n)
    f = np.arange(1, (n - 1) // 2 + 1)
    ang = 2.0 * np.pi * ((f[:, None] * o[None, :]) % n) / n
    rows[1:2 * len(f):2] = np.sqrt(2.0 / n) * np.cos(ang)
    rows[2:2 * len(f) + 1:2] = np.sqrt(2.0 / n) * np.sin(ang)
    rows[n - 1] = np.where(o % 2 == 0, 1.0, -1.0) / np.sqrt(n)
    return rows.astype(np.float32)


def kernel(**inputs):
    import concourse.bacc as _bacc
    from concourse.bass_utils import run_bass_kernel_spmd as _run

    a = {k: np.asarray(v) for k, v in inputs.items()}
    x = a["x"]
    ctx = [np.concatenate([np.full((BATCH, s), VOCAB, x.dtype), x[:, :SEQ - s]], axis=1) for s in (3, 2, 1, 0)]
    ctx = np.stack(ctx, axis=-1).reshape(CHUNKS, TPC, P, ORDER).transpose(2, 0, 1, 3).reshape(P, CHUNKS, TPC * ORDER)
    tok = a["L0_tok_W"].T.reshape(ORDER, VOCAB + 1, VOCAB)
    b_qkv = a["L0_attn_b_qkv"]
    order = np.arange(P)
    arrays = {"x_ctx": ctx}
    arrays.update({f"tok_table{k}": tok[k] for k in range(ORDER)})
    arrays.update({
        "tok_b": a["L0_tok_b"],
        "w_qkv_t": a["L0_attn_w_qkv"].T,
        "b_qk": b_qkv[:Q_DIM + KV_DIM].reshape(QK_TILES, P).T,
        "b_v": b_qkv[Q_DIM + KV_DIM:],
        "w_o_t": a["L0_attn_w_o"].T,
        "b_o": a["L0_attn_b_o"],
        "w_base_t": a["L0_ffn_W_base"].T,
        "b_base": a["L0_ffn_b_base"],
        "enc": np.concatenate([a["L0_ffn_enc0"], a["L0_ffn_enc1"]], axis=0),
        "coefs": np.concatenate([a["L0_ffn_coefs0"], a["L0_ffn_coefs1"]], axis=2),
        "mask": np.concatenate([a["L0_ffn_mask0"], a["L0_ffn_mask1"]], axis=2),
        "rope": rope_table(),
        "fourier_t": fourier_matrix_t(),
        "ident": np.eye(P, dtype=np.float32),
        "mask_qk": np.where(order[None, :] > order[:, None], MASKED, 0.0).astype(np.float32),
        "mask_kq": np.where(order[None, :] < order[:, None], MASKED, 0.0).astype(np.float32),
    })
    nc = _bacc.Bacc("TRN2", target_bir_lowering=False, num_devices=1)
    maps, args = {}, []
    for name, value in arrays.items():
        value = np.ascontiguousarray(value)
        maps[f"in_{name}"] = value
        args.append(nc.dram_tensor(f"in_{name}", value.shape, mybir.dt.from_np(value.dtype), kind="ExternalInput").ap())
    args.append(nc.dram_tensor("out_dram", (TOKENS, D), F32, kind="ExternalOutput").ap())
    build(nc, *args)
    r = _run(nc, [maps], core_ids=[0])
    return r.results[0]["out_dram"].reshape(BATCH, SEQ, D)
```

```python
from contextlib import ExitStack

import numpy as np

import concourse.bass as bass
from concourse import mybir

P = 128
F32 = mybir.dt.float32
F32R = mybir.dt.float32r
I32 = mybir.dt.int32
U8 = mybir.dt.uint8
ALU = mybir.AluOpType
ACT = mybir.ActivationFunctionType
AX = mybir.AxisListType.X

BATCH, SEQ, D, VOCAB, ORDER = 2, 2048, 1024, 1024, 4
HEADS, KV_HEADS, HD = 32, 8, 32
GROUP = HEADS // KV_HEADS
Q_DIM, KV_DIM = HEADS * HD, KV_HEADS * HD
QKV_DIM = Q_DIM + 2 * KV_DIM
EPS = 1e-5
R0, R1, E = 32, 8, 3
R = R0 + R1
SCALING = 16.0 / 32.0
DC = D // P
TOKENS = BATCH * SEQ
CT = 512
CHUNKS = TOKENS // CT
TPC = CT // P
QK_TILES = (Q_DIM + KV_DIM) // P
Q_TILES = Q_DIM // P
TILES = TOKENS // P
VW = 3 * HD
QT = SEQ // P
QC = SEQ // CT
ALL_HEADS = BATCH * HEADS
GROUPS = ALL_HEADS // GROUP
MASKED = -1e30
K_ROWS, M_ROW = 96, 96


class Steps:

    def __init__(self, eng, sem, base):
        self.eng, self.sem, self.at = eng, sem, base

    def do(self, ins):
        self.at = self.at + 1
        ins.then_inc(self.sem, 1)
        self.eng.wait_ge(self.sem, self.at)


def pass_waits(eng, passed):
    eng.sem_inc(passed, 1)


def part_a(nc, x_ctx, tables, tok_b, w_qkv_t, b_qk, b_v, rope, h_dram, q_hi, q_lo, k_hi, k_lo, v_dram, ident_in):
    with ExitStack() as ctx:
        sb = lambda n, s, d: ctx.enter_context(nc.sbuf_tensor(n, s, d))
        sem = lambda n: ctx.enter_context(nc.semaphore(n))
        w_hi = sb("w_hi", [P, DC, QKV_DIM], F32R)
        w_lo = sb("w_lo", [P, DC, QKV_DIM], F32R)
        x_hi = sb("x_hi", [P, DC, CT], F32R)
        x_lo = sb("x_lo", [P, DC, CT], F32R)
        hbuf = sb("hbuf", [P, TPC, D], F32)
        xn = sb("xn", [P, TPC, D], F32)
        tab = sb("tab", [P, 2, CT], F32)
        qf = sb("qf", [P, 2, CT], F32)
        qsw = sb("qsw", [P, 2, CT], F32)
        qrot = sb("qrot", [P, 2, CT], F32)
        rot_hi = sb("rot_hi", [P, 2, CT], F32R)
        rot_lo = sb("rot_lo", [P, 2, CT], F32R)
        vf = sb("vf", [P, 2, KV_DIM], F32)
        vt = sb("vt", [P, 2, KV_HEADS, VW], F32R)
        tokb = sb("tokb", [P, D], F32)
        bqk = sb("bqk", [P, QK_TILES], F32)
        bv = sb("bv", [P, KV_DIM], F32)
        ident = sb("ident", [P, P], F32)
        idx_all = sb("idx_all", [P, CHUNKS, TPC * ORDER], I32)
        idx = sb("idx", [P, TPC * ORDER], I32)
        stats = sb("stats", [P, 2, 6], F32)
        mv = sb("mv", [P, 2], F32)
        var = sb("var", [P, 1], F32)
        std = sb("std", [P, 1], F32)
        rstd = sb("rstd", [P, 1], F32)
        w_in = hbuf[:].rearrange("p t d -> p (t d)")[:, 0:2 * QKV_DIM].rearrange("p (s n) -> p s n", s=2)
        tr_ps = ctx.enter_context(nc.psum_tensor("tr_ps", [P, 2, DC, P], F32))
        qk_ps = ctx.enter_context(nc.psum_tensor("qk_ps", [P, 2, CT], F32))
        v_ps = ctx.enter_context(nc.psum_tensor("v_ps", [P, 2, 512], F32))

        consts = sem("consts")
        w_loaded = [sem(f"w_loaded{s}") for s in range(2)]
        w_hi_done, w_lo_done = sem("w_hi_done"), sem("w_lo_done")
        idx_loaded, idx_copied = sem("idx_loaded"), sem("idx_copied")
        gathered = [sem(f"gathered{t}") for t in range(TPC)]
        h_ready, h_stored = sem("h_ready"), sem("h_stored")
        ln_step, var_ready, std_ready = sem("ln_step"), sem("var_ready"), sem("std_ready")
        xn_ready, tr_ready = sem("xn_ready"), sem("tr_ready")
        x_hi_done, x_lo_done = sem("x_hi_done"), sem("x_lo_done")
        qk_ready, qf_done = sem("qk_ready"), sem("qf_done")
        rot_step, rot_done = sem("rot_step"), sem("rot_done")
        rhi_done, rlo_done = sem("rhi_done"), sem("rlo_done")
        rot_stored = [sem(f"rot_stored{s}") for s in range(2)]
        tab_loaded, ones_set = sem("tab_loaded"), sem("ones_set")
        dve_passed, pool_passed = sem("dve_passed"), sem("pool_passed")
        v_ready, v_done = sem("v_ready"), sem("v_done")
        v_hi_done, v_lo_done = sem("v_hi_done"), sem("v_lo_done")
        v_stored = [sem(f"v_stored{s}") for s in range(2)]
        EMPTY = 16
        AHEAD = 2
        block = ctx.enter_context(nc.Block())

        @block.sync
        def _(sp):
            sp.dma_start(idx_all[:], x_ctx).then_inc(idx_loaded, 16)
            sp.dma_start(ident[:], ident_in).then_inc(consts, 16)
            sp.dma_start(tokb[:], tok_b.rearrange("(a d) -> a d", a=1).broadcast_to([P, D])).then_inc(consts, 16)
            sp.dma_start(bqk[:], b_qk).then_inc(consts, 16)
            sp.dma_start(bv[:], b_v.rearrange("(a d) -> a d", a=1).broadcast_to([P, KV_DIM])).then_inc(consts, 16)
            for c in range(DC):
                if c >= 2:
                    sp.wait_ge(w_lo_done, c - 1)
                sp.dma_start(w_in[:, c % 2, :], w_qkv_t[c * P:(c + 1) * P, :]).then_inc(w_loaded[c % 2], 16)
            sp.dma_start(tab[:], rope[0]).then_inc(tab_loaded, 16)

            def store_h(m):
                for t in range(TPC):
                    sp.wait_ge(h_ready, m * TPC + t + 1)
                    sp.dma_start(h_dram[bass.ds(m * CT + t * P, P), :], hbuf[:, t, :]).then_inc(h_stored, 16)

            def store_rotated(n, f):
                sp.wait_ge(rlo_done, n * QK_TILES + f + 1)
                hi, lo, row = (q_hi, q_lo, f * P) if f < Q_TILES else (k_hi, k_lo, (f - Q_TILES) * P)
                at = (slice(None), bass.ds((n % QC) * CT, CT))
                for dst, src in ((hi, rot_hi), (lo, rot_lo)):
                    dst_rows = dst[bass.ds((n // QC) * (Q_DIM if f < Q_TILES else KV_DIM) + row, P), :]
                    sp.dma_start(dst_rows[at], src[:, f % 2, :].bitcast(F32)).then_inc(rot_stored[f % 2], 16)

            def chunk(n, last):
                for f in range(QK_TILES):
                    store_rotated(n, f)
                    if not last and f == QK_TILES - 1:
                        store_h(n + 1)
                if not last:
                    sp.wait_ge(rot_done, (n + 1) * QK_TILES + AHEAD)
                    sp.dma_start(tab[:], rope[n + 1]).then_inc(tab_loaded, 16)
                for t in range(TPC):
                    sp.wait_ge(v_lo_done, n * TPC + t + 1 + AHEAD)
                    to = v_dram[bass.ds((n // QC) * KV_HEADS, KV_HEADS), :, bass.ds((n % QC) * TPC + t, 1), :]
                    sp.dma_start(to.rearrange("g p a w -> p g (a w)"),
                                 vt[:, t % 2, :, :].bitcast(F32)).then_inc(v_stored[t % 2], 16)

            store_h(0)
            with sp.Fori(0, CHUNKS - 1) as n:
                chunk(n, False)
            chunk(CHUNKS - 1, True)
            sp.wait_ge(h_stored, 16 * TILES)
            for s in range(2):
                sp.wait_ge(rot_stored[s], EMPTY + 16 * CHUNKS * QK_TILES)
                sp.wait_ge(v_stored[s], EMPTY + 16 * CHUNKS * TPC // 2)

        @block.gpsimd
        def _(pool):
            pool.wait_ge(idx_loaded, 16)
            pool.wait_ge(w_lo_done, DC)

            def gather(m, first):
                nc.gpsimd.tensor_copy(idx[:], idx_all[:, m, :] if first else
                                      idx_all[:, bass.ds(m, 1), :].rearrange("p a k -> p (a k)")
                                      ).then_inc(idx_copied, 1)
                pool.wait_ge(idx_copied, m + 1)
                if not first:
                    pool.wait_ge(h_stored, 16 * TPC * m)
                for k in range(ORDER):
                    for t in range(TPC):
                        if k == 0 and not first:
                            pool.wait_ge(xn_ready, m * TPC - TPC + t + 1)
                        if k > 0:
                            pool.wait_ge(gathered[t], 16 * (m * ORDER + k))
                        pass_waits(pool, pool_passed)
                        j = t * ORDER + k
                        nc.gpsimd.indirect_dma_start(
                            hbuf[:, t, :], None, tables[k],
                            bass.IndirectOffsetOnAxis(ap=idx[:, j:j + 1], axis=0),
                            compute_op=ALU.bypass if k == 0 else ALU.add).then_inc(gathered[t], 16)
                for t in range(TPC):
                    pool.wait_ge(gathered[t], 16 * (m + 1) * ORDER)

            gather(0, True)
            with pool.Fori(1, CHUNKS) as m:
                gather(m, False)

        @block.scalar
        def _(act):
            act.sem_inc(qf_done, AHEAD)
            for s in range(2):
                act.sem_inc(rot_stored[s], EMPTY)
                act.sem_inc(v_stored[s], EMPTY)
            for c in range(DC):
                act.wait_ge(w_loaded[c % 2], 16 * (c // 2 + 1))
                nc.scalar.copy(w_hi[:, c, :], w_in[:, c % 2, :]).then_inc(w_hi_done, 1)
            act.wait_ge(consts, 64)

            def deviation(m, t):
                act.wait_ge(var_ready, m * TPC + t + 1)
                nc.scalar.activation(std[:], var[:], ACT.Sqrt).then_inc(std_ready, 1)

            def x_high(m, t):
                act.wait_ge(tr_ready, m * TPC + t + 1)
                nc.scalar.copy(x_hi[:, :, t * P:(t + 1) * P], tr_ps[:, t % 2]).then_inc(x_hi_done, 1)

            def add_bias(n, f):
                act.wait_ge(qk_ready, n * QK_TILES + f + 1)
                act.wait_ge(rot_done, n * QK_TILES + f + 1)
                nc.scalar.activation(qf[:, f % 2, :], qk_ps[:, f % 2, :], ACT.Identity,
                                     bias=bqk[:, f:f + 1]).then_inc(qf_done, 1)

            def rot_high(n, f):
                act.wait_ge(rot_done, n * QK_TILES + f + 1 + AHEAD)
                act.wait_ge(rot_stored[f % 2], EMPTY + 32 * (n * (QK_TILES // 2) + f // 2))
                nc.scalar.copy(rot_hi[:, f % 2, :], qrot[:, f % 2, :]).then_inc(rhi_done, 1)

            def v_high(n, t):
                act.wait_ge(v_done, n * TPC + t + 1 + AHEAD)
                act.wait_ge(v_stored[t % 2], EMPTY + 16 * (n * (TPC // 2) + t // 2))
                nc.scalar.copy(vt[:, t % 2, :, 0:HD], vf[:, t % 2, :].rearrange("p (h w) -> p h w", w=HD)
                               ).then_inc(v_hi_done, 1)

            def chunk(n, last):
                for f in range(QK_TILES):
                    add_bias(n, f)
                    if f >= 1:
                        rot_high(n, f - 1)
                    if f % 2 and f // 2 < TPC and not last:
                        deviation(n + 1, f // 2)
                rot_high(n, QK_TILES - 1)
                for t in range(TPC):
                    v_high(n, t)
                    if not last:
                        x_high(n + 1, t)

            for t in range(TPC):
                deviation(0, t)
            for t in range(TPC):
                x_high(0, t)
            with act.Fori(0, CHUNKS - 1) as n:
                chunk(n, False)
            chunk(CHUNKS - 1, True)

        @block.vector
        def _(dve):
            dve.sem_inc(rot_done, AHEAD)
            dve.sem_inc(v_done, AHEAD)
            dve.sem_inc(v_lo_done, AHEAD)
            nc.vector.memset(vt[:].bitcast(F32), 1.0).then_inc(ones_set, 1)
            for c in range(DC):
                dve.wait_ge(w_hi_done, c + 1)
                nc.vector.tensor_tensor(w_lo[:, c, :], w_in[:, c % 2, :], w_hi[:, c, :].bitcast(F32),
                                        ALU.subtract).then_inc(w_lo_done, 1)
            dve.wait_ge(ones_set, 1)
            dve.wait_ge(consts, 64)
            LN_STEPS, ROT_STEPS = 6, 3

            def layer_norm(m, t):
                at = m * TPC + t
                step = Steps(dve, ln_step, at * LN_STEPS)
                h = hbuf[:, t, :]
                dve.wait_ge(gathered[t], 16 * ORDER * (m + 1))
                nc.vector.tensor_tensor(h, h, tokb[:], ALU.add).then_inc(h_ready, 1)
                dve.wait_ge(h_ready, at + 1)
                step.do(nc.vector.bn_stats(stats[:, 0, :], h[:, 0:512]))
                step.do(nc.vector.bn_stats(stats[:, 1, :], h[:, 512:1024]))
                pass_waits(dve, dve_passed)
                step.do(nc.vector.bn_aggr(mv[:], stats[:].rearrange("p a s -> p (a s)")))
                nc.vector.tensor_scalar(var[:], mv[:, 1:2], EPS, None, ALU.add).then_inc(var_ready, 1)
                dve.wait_ge(std_ready, at + 1)
                step.do(nc.vector.reciprocal(rstd[:], std[:]))
                if not (isinstance(m, int) and m == 0):
                    dve.wait_ge(tr_ready, at - TPC + 1)
                nc.vector.tensor_scalar(xn[:, t, :], h, mv[:, 0:1], rstd[:], ALU.subtract,
                                        ALU.mult).then_inc(xn_ready, 1)
                dve.wait_ge(xn_ready, at + 1)
                step.do(nc.vector.tensor_copy(var[:], rstd[:]))
                step.do(nc.vector.tensor_copy(var[:], rstd[:]))

            def x_low(m, t):
                dve.wait_ge(x_hi_done, m * TPC + t + 1)
                sl = slice(t * P, (t + 1) * P)
                nc.vector.tensor_tensor(x_lo[:, :, sl], tr_ps[:, t % 2], x_hi[:, :, sl].bitcast(F32),
                                        ALU.subtract).then_inc(x_lo_done, 1)

            swap = [i ^ 1 for i in range(32)]

            def rotate(n, f):
                at = n * QK_TILES + f
                step = Steps(dve, rot_step, at * ROT_STEPS)
                s = f % 2
                dve.wait_ge(qf_done, at + 1 + AHEAD)
                if f == 0:
                    dve.wait_ge(tab_loaded, 16 * (n + 1))
                pass_waits(dve, dve_passed)
                step.do(nc.vector.stream_shuffle(qsw[:, s, :], qf[:, s, :], swap))
                step.do(nc.vector.tensor_tensor(qsw[:, s, :], qsw[:, s, :], tab[:, 1, :], ALU.mult))
                step.do(nc.vector.tensor_tensor(qrot[:, s, :], qf[:, s, :], tab[:, 0, :], ALU.mult))
                nc.vector.tensor_tensor(qrot[:, s, :], qrot[:, s, :], qsw[:, s, :], ALU.add).then_inc(rot_done, 1)

            def rot_low(n, f):
                dve.wait_ge(rhi_done, n * QK_TILES + f + 1)
                nc.vector.tensor_tensor(rot_lo[:, f % 2, :], qrot[:, f % 2, :], rot_hi[:, f % 2, :].bitcast(F32),
                                        ALU.subtract).then_inc(rlo_done, 1)

            def values(n, t):
                dve.wait_ge(v_ready, n * TPC + t + 1)
                dve.wait_ge(v_lo_done, n * TPC + t + 1)
                nc.vector.tensor_tensor(vf[:, t % 2, :], v_ps[:, t % 2, 0:KV_DIM], bv[:], ALU.add
                                        ).then_inc(v_done, 1)

            def v_low(n, t):
                dve.wait_ge(v_hi_done, n * TPC + t + 1)
                nc.vector.tensor_tensor(vt[:, t % 2, :, HD:2 * HD], vf[:, t % 2, :].rearrange("p (h w) -> p h w", w=HD),
                                        vt[:, t % 2, :, 0:HD].bitcast(F32), ALU.subtract).then_inc(v_lo_done, 1)

            def chunk(n, last):
                for f in range(QK_TILES):
                    rotate(n, f)
                    if f >= 1:
                        rot_low(n, f - 1)
                    if f % 2 and f // 2 < TPC and not last:
                        layer_norm(n + 1, f // 2)
                rot_low(n, QK_TILES - 1)
                for t in range(TPC):
                    values(n, t)
                    if not last:
                        x_low(n + 1, t)
                    v_low(n, t)

            for t in range(TPC):
                layer_norm(0, t)
            for t in range(TPC):
                x_low(0, t)
            with dve.Fori(0, CHUNKS - 1) as n:
                chunk(n, False)
            chunk(CHUNKS - 1, True)

        @block.tensor
        def _(pe):
            pe.wait_ge(consts, 64)
            pe.wait_ge(w_lo_done, DC)

            def transpose(m, t):
                at = m * TPC + t
                pe.wait_ge(xn_ready, at + 1)
                if not (isinstance(m, int) and m == 0 and t < 2):
                    pe.wait_ge(x_lo_done, at - 1)
                for c in range(DC):
                    mm = nc.tensor.transpose(tr_ps[:, t % 2, c, :], xn[:, t, c * P:(c + 1) * P], ident[:])
                mm.then_inc(tr_ready, 1)

            def chunk(n, last):
                pe.wait_ge(x_lo_done, (n + 1) * TPC)
                for f in range(QK_TILES):
                    pe.wait_ge(qf_done, n * QK_TILES + f + 1)
                    for c in range(DC):
                        w = (w_hi[:, c, f * P:(f + 1) * P], w_lo[:, c, f * P:(f + 1) * P])
                        x = (x_hi[:, c, :], x_lo[:, c, :])
                        for k, (a, b) in enumerate(((0, 0), (0, 1), (1, 0))):
                            mm = nc.tensor.matmul(qk_ps[:, f % 2, :], w[a], x[b], start=(c == 0 and k == 0),
                                                  stop=(c == DC - 1 and k == 2))
                    mm.then_inc(qk_ready, 1)
                for t in range(TPC):
                    pe.wait_ge(v_done, n * TPC + t + 1)
                    for c in range(DC):
                        w = (w_hi[:, c, Q_DIM + KV_DIM:], w_lo[:, c, Q_DIM + KV_DIM:])
                        x = (x_hi[:, c, t * P:(t + 1) * P], x_lo[:, c, t * P:(t + 1) * P])
                        for k, (a, b) in enumerate(((0, 0), (1, 0), (0, 1))):
                            mm = nc.tensor.matmul(v_ps[:, t % 2, 0:KV_DIM], x[b], w[a], start=(c == 0 and k == 0),
                                                  stop=(c == DC - 1 and k == 2))
                    mm.then_inc(v_ready, 1)
                    if not last:
                        transpose(n + 1, t)

            for t in range(TPC):
                transpose(0, t)
            with pe.Fori(0, CHUNKS - 1) as n:
                chunk(n, False)
            chunk(CHUNKS - 1, True)


def score_units():
    return [(c, kt, max(0, kt - c * TPC)) for c in range(QC) for kt in range(TPC * (c + 1))]


def max_units():
    return [(i, j, CT if j < i // TPC else (i % TPC + 1) * P) for i in range(QT) for j in range(i // TPC + 1)]


UNITS, MAXES = score_units(), max_units()
NU, NM = len(UNITS), len(MAXES)
LAST_OF = [max(u for u, (c, _, _) in enumerate(UNITS) if c == k) for k in range(QC)]
HIGH, LOW, LAG = 3, 4, 8
TURN = 33
SLOTS = 10
HIGH_DVE = [u for u in range(NU) if u % 5 == 1]
LOW_DVE = [u for u in range(NU) if u % 10 in (0, 3, 7)]
LOW_POOL = [u for u in range(NU) if u not in LOW_DVE]
SCORE_BANKS, MAX_BANKS = 4, 2


def vector_work(width):
    return width + 60


def maxima_after():
    width = [CT - j * P for _, _, j in UNITS]
    order = [(TURN + k) % NU for k in range(NU)]
    fixed = {}
    for u in range(NU):
        w = vector_work(width[u - HIGH]) // 2 if (u - HIGH) % NU in HIGH_DVE else 0
        if (u - LOW) % NU in LOW_DVE:
            w += vector_work(width[u - LOW])
        if (u - LAG) % NU in LAST_OF:
            w += vector_work(CT)
        if u in (TURN - 1, TURN + 2):
            w += 3 * CT // 4
        fixed[u] = w
    total = sum(fixed.values()) + sum(vector_work(w) for _, _, w in MAXES)
    columns = sum(vector_work(w) for w in width)
    passed, done, n, counts = 0, 0, 0, {}
    for u in order:
        passed += vector_work(width[u])
        done += fixed[u]
        while n < NM and done + vector_work(MAXES[n][2]) / 2 <= total * passed / columns:
            done += vector_work(MAXES[n][2])
            n += 1
        counts[u] = NM if u == TURN - 1 else n
    return counts


MAXES_AFTER = maxima_after()
EARLY = MAXES_AFTER[NU - 1]


def head_plan(first, more, two_more):
    plan, n = [], EARLY
    for u in range(NU if more else NU + LAG):
        if u < NU:
            plan.append(("score", u, 0))
        if u == TURN + 2 and more:
            plan.append(("rows", 0, 0))
        for what, lag in (("high", HIGH), ("low", LOW)):
            if 0 <= u - lag < NU:
                plan.append((what, u - lag, 0))
            elif u < lag and not first:
                plan.append((what, NU + u - lag, 1))
        if u == TURN:
            n = 0
        while u < NU and n < MAXES_AFTER[u]:
            if two_more if u >= TURN else more:
                plan.append(("max", n, -2 if u >= TURN else -1))
            n += 1
            if n == NM and more:
                plan.append(("all_max", 0, 0))
        if u >= LAG:
            plan.append(("value", u - LAG, 0))
        elif not first:
            plan.append(("value", NU + u - LAG, 1))
        if u == TURN and more:
            plan.append(("turn", 0, 0))
    return plan


def part_b(nc, q_hi, q_lo, k_hi, k_lo, v_dram, o_hi_dram, o_lo_dram, den_dram, ident_in, mask_qk, mask_kq):
    with ExitStack() as ctx:
        sb = lambda n, s, d: ctx.enter_context(nc.sbuf_tensor(n, s, d))
        sem = lambda n: ctx.enter_context(nc.semaphore(n))
        qs = [sb(f"qs{s}", [P, SEQ], F32R) for s in range(GROUP)]
        ks = [sb(f"ks{s}", [P, SEQ], F32R) for s in range(2)]
        vs = [sb(f"vs{s}", [P, QT, VW], F32R) for s in range(2)]
        probs = sb("probs", [P, SLOTS, CT], F32)
        p_hi = sb("p_hi", [P, SLOTS, CT], F32R)
        p_lo = sb("p_lo", [P, SLOTS, CT], F32R)
        o_sb = sb("o_sb", [VW, 2, SEQ], F32)
        mpart = sb("mpart", [P, QT, QC], F32)
        mcol = sb("mcol", [P, QT], F32)
        m_hi = sb("m_hi", [QT, P], F32R)
        m_lo = sb("m_lo", [QT, P], F32R)
        ident = sb("ident_b", [P, P], F32)
        consts_in = sb("consts_in", [P, 3, P], F32)
        consts_r = sb("consts_r", [P, 3, P], F32R)
        identr, mqk, mkq = (consts_r[:, j, :] for j in range(3))
        st_ps = ctx.enter_context(nc.psum_tensor("st_ps", [P, SCORE_BANKS, CT], F32))
        mx_ps = ctx.enter_context(nc.psum_tensor("mx_ps", [P, MAX_BANKS, CT], F32))
        o_ps = ctx.enter_context(nc.psum_tensor("o_ps", [P, 2, CT], F32))
        mt_ps = o_ps[0:QT, 0, 0:P]

        q_loaded = [sem(f"q_loaded{s}") for s in range(GROUP)]
        kv_loaded = [sem(f"kv_loaded{s}") for s in range(2)]
        consts, consts_done, ones_done = sem("consts_b"), sem("consts_done"), sem("ones_done")
        max_ready, max_done, max_all = sem("max_ready"), sem("max_done"), sem("max_all")
        turned, m_hi_done, m_lo_done, m_rows = sem("turned"), sem("m_hi_done"), sem("m_lo_done"), sem("m_rows")
        st_ready, exp_done, hi_done = sem("st_ready"), sem("exp_done"), sem("hi_done")
        lo_dve_done, lo_pool_done = sem("lo_dve_done"), sem("lo_pool_done")
        pv_done, o_done = sem("pv_done"), sem("o_done")
        o_stored = [sem(f"o_stored{s}") for s in range(2)]
        P_FREE, O_FREE = SLOTS, 2
        EMPTY = 16
        Q_LOAD, KV_LOAD, STORE = 3 * 16, 4 * 16, 3 * 16
        block = ctx.enter_context(nc.Block())

        def kv_of(s):
            return 0 if s == 0 else 1

        def max_k_of(s):
            return 0 if s < 2 else 1

        def lo_done(h, u):
            if u in LOW_POOL:
                return lo_pool_done, h * len(LOW_POOL) + LOW_POOL.index(u) + 1
            return lo_dve_done, h * len(LOW_DVE) + LOW_DVE.index(u) + 1

        def maxima_before(eng, g, reg):
            if isinstance(g, int):
                return g * (GROUP * NM)
            eng.reg_mul(reg, g, GROUP * NM)
            return eng.snap(reg)

        def split_ready(h, u):
            if u in HIGH_DVE:
                return hi_done, h * len(HIGH_DVE) + HIGH_DVE.index(u) + 1
            return exp_done, h * NU + u + 1

        def groups(eng, group):
            group(0, True, False)
            with eng.Fori(1, GROUPS - 1) as g:
                group(g, False, False)
            group(GROUPS - 1, False, True)

        def heads(g, first, last):
            return [(g * GROUP + s, s, head_plan(first and s == 0, not (last and s == GROUP - 1),
                                                 not (last and s >= GROUP - 2))) for s in range(GROUP)]

        @block.sync
        def _(sp):
            for j, a in enumerate((ident_in, mask_qk, mask_kq)):
                sp.dma_start(consts_in[:, j, :], a).then_inc(consts, 16)
            sp.dma_start(ident[:], ident_in).then_inc(consts, 16)

            def load_q(g, s):
                row = g * (GROUP * HD) + s * HD
                for r, q in enumerate((q_hi, q_hi, q_lo)):
                    sp.dma_start(qs[s][r * HD:(r + 1) * HD, :].bitcast(F32), q[bass.ds(row, HD), :]
                                 ).then_inc(q_loaded[s], 16)

            def load_kv(g, b):
                for r, k in enumerate((k_hi, k_lo, k_hi)):
                    sp.dma_start(ks[b][r * HD:(r + 1) * HD, :].bitcast(F32), k[bass.ds(g * HD, HD), :]
                                 ).then_inc(kv_loaded[b], 16)
                sp.dma_start(vs[b][:].bitcast(F32), v_dram[bass.ds(g, 1)].rearrange("a p t w -> (a p) t w")
                             ).then_inc(kv_loaded[b], 16)

            def store(g, s):
                h = g * GROUP + s
                sp.wait_ge(o_done, O_FREE + (h + 1) * QC)
                for r, dst in enumerate((o_hi_dram, o_lo_dram, den_dram)):
                    sp.dma_start(dst[bass.ds(h * HD, HD), :], o_sb[r * HD:(r + 1) * HD, s % 2, :]
                                 ).then_inc(o_stored[s % 2], 16)

            def send_rows(h, s):
                for r, (m, done) in enumerate(((m_hi, m_hi_done), (m_lo, m_lo_done))):
                    sp.wait_ge(done, h + 1)
                    sp.dma_start(qs[s][M_ROW + r:M_ROW + r + 1, :].bitcast(F32).rearrange("a (t p) -> a t p", p=P),
                                 m[:].bitcast(F32)).then_inc(m_rows, 16)

            def group(g, last):
                for s in range(GROUP):
                    if not (last and s == GROUP - 1):
                        send_rows(g * GROUP + s + 1, (s + 1) % GROUP)
                    store(g, s)
                    if last:
                        continue
                    sp.wait_ge(pv_done, P_FREE + (g * GROUP + s + 1) * NU)
                    load_q(g + 1, s)
                    if s == 1:
                        load_kv(g + 1, 0)
                    if s == GROUP - 1:
                        load_kv(g + 1, 1)

            load_q(0, 0)
            load_kv(0, 0)
            load_q(0, 1)
            load_kv(0, 1)
            load_q(0, 2)
            load_q(0, 3)
            send_rows(0, 0)
            with sp.Fori(0, GROUPS - 1) as g:
                group(g, False)
            group(GROUPS - 1, True)
            for s in range(2):
                sp.wait_ge(o_stored[s], EMPTY + STORE * ALL_HEADS // 2)

        @block.gpsimd
        def _(pool):
            pool.wait_ge(consts, 64)
            nc.gpsimd.tensor_copy(consts_r[:], consts_in[:]).then_inc(consts_done, 1)

            def low(h, u):
                w = CT - UNITS[u][2] * P
                pool.wait_ge(*split_ready(h, u))
                nc.gpsimd.tensor_tensor(p_lo[:, u % SLOTS, 0:w], probs[:, u % SLOTS, 0:w],
                                        p_hi[:, u % SLOTS, 0:w].bitcast(F32), ALU.subtract).then_inc(lo_pool_done, 1)

            def group(g, first, last):
                for h, s, plan in heads(g, first, last):
                    for what, u, back in plan:
                        if what == "low" and u in LOW_POOL:
                            low(h - back, u)

            groups(pool, group)

        @block.scalar
        def _(act):
            for s in range(2):
                act.sem_inc(o_stored[s], EMPTY)

            def exps(h, u):
                w = CT - UNITS[u][2] * P
                act.wait_ge(st_ready, h * NU + u + 1)
                act.wait_ge(pv_done, h * NU + u + 1)
                if u not in HIGH_DVE:
                    nc.scalar.activation(p_hi[:, u % SLOTS, 0:w], st_ps[:, u % SCORE_BANKS, 0:w], ACT.Exp,
                                         scale=float(HD) ** -0.5)
                nc.scalar.activation(probs[:, u % SLOTS, 0:w], st_ps[:, u % SCORE_BANKS, 0:w], ACT.Exp,
                                     scale=float(HD) ** -0.5).then_inc(exp_done, 1)

            def group(g, first, last):
                for h, s, plan in heads(g, first, last):
                    for what, u, back in plan:
                        if what == "score":
                            exps(h, u)

            groups(act, group)

        @block.vector
        def _(dve):
            max_count = dve.alloc_register("max_count")
            dve.sem_inc(pv_done, P_FREE)
            dve.sem_inc(o_done, O_FREE)
            for s in range(2):
                nc.vector.memset(ks[s][M_ROW:P, :].bitcast(F32), 1.0).then_inc(ones_done, 1)

            def row_max(h, before, n):
                i, j, w = MAXES[n]
                dve.wait_ge(max_ready, before + n + 1)
                if n == 0 and not (isinstance(h, int) and h == 0):
                    dve.wait_ge(max_all, h)
                nc.vector.tensor_reduce(mpart[:, i, j:j + 1], mx_ps[:, n % MAX_BANKS, 0:w], AX, ALU.max
                                        ).then_inc(max_done, 1)

            def all_max(before):
                dve.wait_ge(max_done, before + NM)
                for g in range(QC):
                    last = nc.vector.tensor_reduce(mcol[:, g * TPC:(g + 1) * TPC],
                                                   mpart[:, g * TPC:(g + 1) * TPC, 0:g + 1], AX, ALU.max)
                last.then_inc(max_all, 1)

            def maxima_rows(h):
                dve.wait_ge(turned, h + 1)
                if not (isinstance(h, int) and h == 0):
                    dve.wait_ge(m_rows, 32 * h)
                nc.vector.tensor_scalar(m_hi[:], mt_ps, -1.0, None, ALU.mult).then_inc(m_hi_done, 1)
                dve.wait_ge(m_hi_done, h + 1)
                nc.vector.scalar_tensor_tensor(m_lo[:], mt_ps, -1.0, m_hi[:].bitcast(F32),
                                               ALU.mult, ALU.subtract).then_inc(m_lo_done, 1)

            def high(h, u):
                w = CT - UNITS[u][2] * P
                dve.wait_ge(exp_done, h * NU + u + 1)
                nc.vector.tensor_copy(p_hi[:, u % SLOTS, 0:w], probs[:, u % SLOTS, 0:w]).then_inc(hi_done, 1)

            def low(h, u):
                w = CT - UNITS[u][2] * P
                dve.wait_ge(*split_ready(h, u))
                nc.vector.tensor_tensor(p_lo[:, u % SLOTS, 0:w], probs[:, u % SLOTS, 0:w],
                                        p_hi[:, u % SLOTS, 0:w].bitcast(F32), ALU.subtract).then_inc(lo_dve_done, 1)

            def take(h, c, slot, stores_before):
                dve.wait_ge(pv_done, P_FREE + h * NU + LAST_OF[c] + 1)
                if c == 0:
                    dve.wait_ge(o_stored[slot], EMPTY + STORE * stores_before)
                nc.vector.tensor_copy(o_sb[:, slot, c * CT:(c + 1) * CT], o_ps[0:VW, c % 2, :]).then_inc(o_done, 1)

            def group(g, first, last):
                before_group = maxima_before(dve, g, max_count)
                for h, s, plan in heads(g, first, last):
                    for what, u, back in plan:
                        if what == "max":
                            row_max(h - back, before_group + (s - back) * NM, u)
                        if what == "all_max":
                            all_max(before_group + (s + 1) * NM)
                        if what == "rows":
                            maxima_rows(h + 1)
                        if what == "high" and u in HIGH_DVE:
                            high(h - back, u)
                        if what == "low" and u in LOW_DVE:
                            low(h - back, u)
                        if what == "value" and u in LAST_OF:
                            at = s - back
                            take(h - back, LAST_OF.index(u), at % 2, g * (GROUP // 2) + (at - at % 2) // 2)

            for n in range(NM):
                row_max(0, 0, n)
            all_max(0)
            for n in range(EARLY):
                row_max(1, NM, n)
            maxima_rows(0)
            groups(dve, group)

        @block.tensor
        def _(pe):
            max_count = pe.alloc_register("max_count")
            pe.wait_ge(consts_done, 1)
            pe.wait_ge(ones_done, 2)

            def row_scores(g, h, s, before, n):
                i, j, w = MAXES[n]
                if n == 0:
                    pe.wait_ge(q_loaded[s], Q_LOAD * (g + 1))
                    if s == 0:
                        pe.wait_ge(kv_loaded[0], KV_LOAD * (g + 1))
                    if s == 2:
                        pe.wait_ge(kv_loaded[1], KV_LOAD * (g + 1))
                if not (isinstance(h, int) and h == 0 and n < MAX_BANKS):
                    pe.wait_ge(max_done, before + (n - (MAX_BANKS - 1)))
                diagonal = j == i // TPC
                out = mx_ps[:, n % MAX_BANKS, 0:w]
                mm = nc.tensor.matmul(out, qs[s][0:K_ROWS, i * P:(i + 1) * P],
                                      ks[max_k_of(s)][0:K_ROWS, j * CT:j * CT + w], start=True, stop=not diagonal)
                if diagonal:
                    mm = nc.tensor.matmul(out[:, w - P:w], identr, mqk, start=False, stop=True)
                mm.then_inc(max_ready, 1)

            def turn(h):
                pe.wait_ge(max_all, h + 1)
                if not (isinstance(h, int) and h == 0):
                    pe.wait_ge(o_done, O_FREE + (h - 1) * QC + QC - 1)
                nc.tensor.transpose(mt_ps, mcol[:], ident[:]).then_inc(turned, 1)

            def scores(g, h, s, u):
                c, kt, j = UNITS[u]
                w = CT - j * P
                if u == 0:
                    pe.wait_ge(m_rows, 32 * (h + 1))
                    if s == 1:
                        pe.wait_ge(kv_loaded[1], KV_LOAD * (g + 1))
                if not (isinstance(h, int) and h == 0 and u < SCORE_BANKS):
                    pe.wait_ge(exp_done, h * NU + u - (SCORE_BANKS - 1))
                diagonal = kt >= c * TPC
                mm = nc.tensor.matmul(st_ps[:, u % SCORE_BANKS, 0:w], ks[kv_of(s)][0:M_ROW + 2, kt * P:(kt + 1) * P],
                                      qs[s][0:M_ROW + 2, c * CT + j * P:(c + 1) * CT], start=True, stop=not diagonal)
                if diagonal:
                    mm = nc.tensor.matmul(st_ps[:, u % SCORE_BANKS, 0:P], identr, mkq, start=False, stop=True)
                mm.then_inc(st_ready, 1)

            def values(h, s, u):
                c, kt, j = UNITS[u]
                w = CT - j * P
                out = o_ps[0:VW, c % 2, j * P:CT]
                pe.wait_ge(*lo_done(h, u))
                if kt == 0:
                    pe.wait_ge(o_done, h * QC + c + 1)
                v = vs[kv_of(s)][:, kt, :]
                nc.tensor.matmul(out, v, p_hi[:, u % SLOTS, 0:w], start=(kt == 0), stop=False)
                nc.tensor.matmul(out, v, p_lo[:, u % SLOTS, 0:w], start=False,
                                 stop=(u in LAST_OF)).then_inc(pv_done, 1)

            def group(g, first, last):
                before_group = maxima_before(pe, g, max_count)
                for h, s, plan in heads(g, first, last):
                    for what, u, back in plan:
                        if what == "score":
                            scores(g, h, s, u)
                        if what == "value":
                            values(h - back, (s - back) % GROUP, u)
                        if what == "max":
                            at = s - back
                            row_scores(g + at // GROUP, h - back, at % GROUP, before_group + at * NM, u)
                        if what == "turn":
                            turn(h + 1)

            for n in range(NM):
                row_scores(0, 0, 0, 0, n)
            turn(0)
            for n in range(EARLY):
                row_scores(0, 1, 1, NM, n)
            groups(pe, group)


def part_c(nc, o_hi_dram, o_lo_dram, den_dram, h_dram, w_o_t, b_o, w_base_t, b_base, enc, coefs, mask, fourier_t,
           ident_in, out):
    with ExitStack() as ctx:
        sb = lambda n, s, d: ctx.enter_context(nc.sbuf_tensor(n, s, d))
        sem = lambda n: ctx.enter_context(nc.semaphore(n))
        w_hi = sb("wc_hi", [P, 2, DC, D], F32R)
        w_lo = sb("wc_lo", [P, 2, DC, D], F32R)
        o_in = sb("o_in", [P, 2, 3, DC, P], F32)
        a_f = sb("a_f", [P, DC, P], F32)
        h_in = sb("h_in", [P, 2, D], F32)
        h1 = sb("h1", [P, 2, D], F32)
        xn = sb("xn_c", [P, D], F32)
        a_hi, a_lo = sb("a_hi", [P, DC, P], F32R), sb("a_lo", [P, DC, P], F32R)
        x_hi, x_lo = sb("xc_hi", [P, DC, P], F32R), sb("xc_lo", [P, DC, P], F32R)
        bo, bb = sb("bo", [P, D], F32), sb("bb", [P, D], F32)
        ident = sb("ident_c", [P, P], F32)
        stats, mv = sb("stats_c", [P, 2, 6], F32), sb("mv_c", [P, 2], F32)
        var, std, rstd = sb("var_c", [P, 1], F32), sb("std_c", [P, 1], F32), sb("rstd_c", [P, 1], F32)
        mk8 = sb("mk8", [P, DC, E, R], U8)
        w_in = o_in[:, :, 0].rearrange("p s c t -> p s (c t)")
        enc_sb = o_in[0:R, 0, 1].rearrange("p c t -> p (c t)")
        tw = o_in[0:R, 0, 2].rearrange("p c t -> p (c t)")
        by_expert = lambda a: a.rearrange("p (c e r) -> p c e r", e=E, r=R)
        cf = by_expert(h1[:].rearrange("p a d -> p (a d)")[:, 0:DC * E * R])
        mkf = by_expert(o_in[:, 1, 1].rearrange("p c t -> p (c t)")[:, 0:DC * E * R])
        wr = xn[:, 0:DC * R].rearrange("p (c r) -> p c r", r=R)
        t2_ps = ctx.enter_context(nc.psum_tensor("t2_ps", [P, DC, P], F32))
        o_ps = ctx.enter_context(nc.psum_tensor("oc_ps", [P, D], F32))
        f_ps = ctx.enter_context(nc.psum_tensor("f_ps", [P, D], F32))

        consts, coefs_in, four_in = sem("consts_c"), sem("coefs_in"), [sem(f"four_in{s}") for s in range(2)]
        w_loaded = [sem(f"wc_loaded{s}") for s in range(2)]
        prep, tw_ps_done, tw_done = sem("prep"), sem("tw_ps_done"), sem("tw_done")
        delta_ready, wsum_done = sem("delta_ready"), sem("wsum_done")
        w_hi_done, w_lo_done = sem("wc_hi_done"), sem("wc_lo_done")
        o_loaded = [sem(f"o_loaded{s}") for s in range(2)]
        h_loaded = [sem(f"h_loaded{s}") for s in range(2)]
        a_sum, recip_done, a_ready = sem("a_sum"), sem("recip_done"), sem("a_ready")
        a_hi_done, a_lo_done = sem("a_hi_done"), sem("a_lo_done")
        hb_done, o_ready, h1_done, h1b_done = sem("hb_done"), sem("o_ready"), sem("h1_done"), sem("h1b_done")
        ln_step, var_ready, std_ready = sem("ln_step_c"), sem("var_ready_c"), sem("std_ready_c")
        xn_ready, t2_ready = sem("xn_ready_c"), sem("t2_ready")
        x_hi_done, x_lo_done, f_ready = sem("xc_hi_done"), sem("xc_lo_done"), sem("f_ready")
        out_done, dve_passed = sem("out_done"), sem("dve_passed_c")
        out_stored = [sem(f"out_stored{s}") for s in range(2)]
        EMPTY = 16
        ONE = 1
        NW = 2 * DC
        block = ctx.enter_context(nc.Block())

        def tiles(eng, tile):
            tile(0, 0, True, False)
            with eng.Fori(0, TILES // 2 - 1) as i:
                for k in range(2):
                    tile(2 * i + 1 + k, 1 - k, False, False)
            tile(TILES - 1, 1, False, True)

        def loads_of(t, s):
            return (t - s) // 2 + 1

        @block.sync
        def _(sp):
            for c in range(DC):
                sp.dma_start(cf[:, c], coefs[:, c * P:(c + 1) * P, :].rearrange("e p r -> p e r")).then_inc(coefs_in, 16)
                sp.dma_start(mk8[:, c], mask[:, c * P:(c + 1) * P, :].rearrange("e p r -> p e r")).then_inc(coefs_in, 16)
            sp.dma_start(enc_sb, enc).then_inc(consts, 16)
            sp.dma_start(ident[:], ident_in).then_inc(consts, 16)
            for dst, b in ((bo, b_o), (bb, b_base)):
                sp.dma_start(dst[:], b.rearrange("(a d) -> a d", a=1).broadcast_to([P, D])).then_inc(consts, 16)
            for c in range(DC):
                if c >= 2:
                    sp.wait_ge(tw_ps_done, c - 1)
                sp.dma_start(h_in[:, c % 2, :], fourier_t[c * P:(c + 1) * P, :]).then_inc(four_in[c % 2], 16)
                if c >= 2:
                    sp.wait_ge(w_lo_done, c - 1)
                sp.dma_start(w_in[:, c % 2, :], w_o_t[c * P:(c + 1) * P, :]).then_inc(w_loaded[c % 2], 16)
            for c in range(DC):
                sp.wait_ge(w_lo_done, DC + c - 1)
                sp.dma_start(w_in[:, c % 2, :], w_base_t[c * P:(c + 1) * P, :]).then_inc(w_loaded[c % 2], 16)

            def load_h(t, s):
                sp.dma_start(h_in[:, s, :], h_dram[bass.ds(t * P, P), :]).then_inc(h_loaded[s], 16)

            def load_o(t, s):
                for r, src in enumerate((o_hi_dram, o_lo_dram, den_dram)):
                    part = src[bass.ds((t // QT) * Q_DIM, Q_DIM), bass.ds((t % QT) * P, P)]
                    sp.dma_start(o_in[:, s, r], part.rearrange("(c p) t -> p c t", p=P)).then_inc(o_loaded[s], 16)

            sp.wait_ge(w_lo_done, NW)
            sp.wait_ge(tw_ps_done, DC)
            sp.wait_ge(delta_ready, DC)
            for t in range(2):
                load_o(t, t)
                load_h(t, t)

            def tile(t, s, first, last):
                if not last:
                    sp.wait_ge(a_ready, t + 1)
                    load_o(t + 2, s)
                    sp.wait_ge(h1_done, t + 1)
                    load_h(t + 2, s)
                sp.wait_ge(out_done, t + 1 + ONE)
                sp.dma_start(out[bass.ds(t * P, P), :], h1[:, s, :]).then_inc(out_stored[s], 16)

            with sp.Fori(0, TILES // 2 - 1) as i:
                for s in range(2):
                    tile(2 * i + s, s, False, False)
            for s in range(2):
                tile(TILES - 2 + s, s, False, True)
            for s in range(2):
                sp.wait_ge(out_stored[s], EMPTY + 16 * TILES // 2)

        @block.gpsimd
        def _(pool):
            pool.wait_ge(consts, 64)

            def join(t, s, first):
                pool.wait_ge(o_loaded[s], 48 * loads_of(t, s))
                if not first:
                    pool.wait_ge(a_lo_done, t)
                nc.gpsimd.tensor_tensor(a_f[:], o_in[:, s, 0], o_in[:, s, 1], ALU.add).then_inc(a_sum, 1)

            def tile(t, s, first, last):
                pool.wait_ge(h_loaded[s], 16 * loads_of(t, s))
                nc.gpsimd.tensor_tensor(h_in[:, s, :], h_in[:, s, :], bo[:], ALU.add).then_inc(hb_done, 1)
                if not last:
                    join(t + 1, 1 - s, False)
                pool.wait_ge(xn_ready, t + 1)
                nc.gpsimd.tensor_tensor(h1[:, s, :], h1[:, s, :], bb[:], ALU.add).then_inc(h1b_done, 1)

            join(0, 0, True)
            tiles(pool, tile)

        @block.scalar
        def _(act):
            for s in range(2):
                act.sem_inc(out_stored[s], EMPTY)
            for c in range(NW):
                l, k = c // DC, c % DC
                if l == 0:
                    act.wait_ge(w_loaded[c % 2], 16 * (c // 2 + 1))
                else:
                    act.wait_ge(wsum_done, k + 1)
                nc.scalar.copy(w_hi[:, l, k, :], w_in[:, c % 2, :]).then_inc(w_hi_done, 1)

            def a_high(t, first):
                act.wait_ge(a_ready, t + 1)
                if not first:
                    act.wait_ge(o_ready, t)
                nc.scalar.copy(a_hi[:], a_f[:]).then_inc(a_hi_done, 1)

            def tile(t, s, first, last):
                act.wait_ge(var_ready, t + 1)
                nc.scalar.activation(std[:], var[:], ACT.Sqrt).then_inc(std_ready, 1)
                if not last:
                    a_high(t + 1, False)
                act.wait_ge(t2_ready, t + 1)
                nc.scalar.copy(x_hi[:], t2_ps[:]).then_inc(x_hi_done, 1)

            a_high(0, True)
            tiles(act, tile)

        @block.vector
        def _(dve):
            dve.sem_inc(out_done, ONE)
            dve.wait_ge(coefs_in, 16 * 2 * DC)
            step = Steps(dve, prep, 0)
            step.do(nc.vector.tensor_copy(mkf, mk8[:]))
            step.do(nc.vector.tensor_tensor(cf, cf, mkf, ALU.mult))
            step.do(nc.vector.tensor_tensor(wr, cf[:, :, 0, :], cf[:, :, 1, :], ALU.add))
            step.do(nc.vector.tensor_tensor(wr, wr, cf[:, :, 2, :], ALU.add))

            def w_low(c):
                dve.wait_ge(w_hi_done, c + 1)
                nc.vector.tensor_tensor(w_lo[:, c // DC, c % DC, :], w_in[:, c % 2, :],
                                        w_hi[:, c // DC, c % DC, :].bitcast(F32), ALU.subtract).then_inc(w_lo_done, 1)

            for c in range(DC):
                w_low(c)
            dve.wait_ge(tw_ps_done, DC)
            nc.vector.tensor_scalar(tw, o_ps[0:R, :], SCALING, None, ALU.mult).then_inc(tw_done, 1)
            for c in range(DC):
                dve.wait_ge(w_loaded[c % 2], 16 * ((DC + c) // 2 + 1))
                dve.wait_ge(delta_ready, c + 1)
                nc.vector.tensor_tensor(w_in[:, c % 2, :], w_in[:, c % 2, :], f_ps[:], ALU.add).then_inc(wsum_done, 1)
                dve.wait_ge(wsum_done, c + 1)
                w_low(DC + c)
            LN_STEPS = 4

            def attended(t, s):
                dve.wait_ge(o_loaded[s], 48 * loads_of(t, s))
                nc.vector.reciprocal(o_in[:, s, 2], o_in[:, s, 2]).then_inc(recip_done, 1)
                dve.wait_ge(recip_done, t + 1)
                dve.wait_ge(a_sum, t + 1)
                nc.vector.tensor_tensor(a_f[:], a_f[:], o_in[:, s, 2], ALU.mult).then_inc(a_ready, 1)

            def a_low(t):
                dve.wait_ge(a_hi_done, t + 1)
                nc.vector.tensor_tensor(a_lo[:], a_f[:], a_hi[:].bitcast(F32), ALU.subtract).then_inc(a_lo_done, 1)

            def finish(t, s):
                dve.wait_ge(f_ready, t + 1)
                dve.wait_ge(h1b_done, t + 1)
                nc.vector.tensor_tensor(h1[:, s, :], f_ps[:], h1[:, s, :], ALU.add).then_inc(out_done, 1)

            def tile(t, s, first, last):
                dve.wait_ge(o_ready, t + 1)
                dve.wait_ge(hb_done, t + 1)
                dve.wait_ge(out_stored[s], EMPTY + 16 * (loads_of(t, s) - 1))
                nc.vector.tensor_tensor(h1[:, s, :], o_ps[:], h_in[:, s, :], ALU.add).then_inc(h1_done, 1)
                dve.wait_ge(h1_done, t + 1)
                st = Steps(dve, ln_step, t * LN_STEPS)
                st.do(nc.vector.bn_stats(stats[:, 0, :], h1[:, s, 0:512]))
                st.do(nc.vector.bn_stats(stats[:, 1, :], h1[:, s, 512:1024]))
                pass_waits(dve, dve_passed)
                st.do(nc.vector.bn_aggr(mv[:], stats[:].rearrange("p a s -> p (a s)")))
                nc.vector.tensor_scalar(var[:], mv[:, 1:2], EPS, None, ALU.add).then_inc(var_ready, 1)
                dve.wait_ge(std_ready, t + 1)
                st.do(nc.vector.reciprocal(rstd[:], std[:]))
                if not first:
                    dve.wait_ge(t2_ready, t)
                nc.vector.tensor_scalar(xn[:], h1[:, s, :], mv[:, 0:1], rstd[:], ALU.subtract,
                                        ALU.mult).then_inc(xn_ready, 1)
                if not last:
                    attended(t + 1, 1 - s)
                    a_low(t + 1)
                if not first:
                    finish(t - 1, 1 - s)
                dve.wait_ge(x_hi_done, t + 1)
                nc.vector.tensor_tensor(x_lo[:], t2_ps[:], x_hi[:].bitcast(F32), ALU.subtract).then_inc(x_lo_done, 1)

            attended(0, 0)
            a_low(0)
            tiles(dve, tile)
            finish(TILES - 1, 1)

        @block.tensor
        def _(pe):
            pe.wait_ge(prep, 4)
            for c in range(DC):
                pe.wait_ge(four_in[c % 2], 16 * (c // 2 + 1))
                for n in range(2):
                    mm = nc.tensor.matmul(o_ps[0:R, n * 512:(n + 1) * 512], wr[:, c, :],
                                          h_in[:, c % 2, n * 512:(n + 1) * 512], start=(c == 0), stop=(c == DC - 1))
                mm.then_inc(tw_ps_done, 1)
            pe.wait_ge(tw_done, 1)
            pe.wait_ge(consts, 64)
            for c in range(DC):
                if c:
                    pe.wait_ge(wsum_done, c)
                for n in range(2):
                    mm = nc.tensor.matmul(f_ps[:, n * 512:(n + 1) * 512], enc_sb[:, c * P:(c + 1) * P],
                                          tw[:, n * 512:(n + 1) * 512], start=True, stop=True)
                mm.then_inc(delta_ready, 1)
            pe.wait_ge(w_lo_done, NW)

            def turn_x(t, first):
                pe.wait_ge(xn_ready, t + 1)
                if not first:
                    pe.wait_ge(x_lo_done, t)
                for c in range(DC):
                    mm = nc.tensor.transpose(t2_ps[:, c, :], xn[:, c * P:(c + 1) * P], ident[:])
                mm.then_inc(t2_ready, 1)

            def product(out_ps, x, l, done):
                for c in range(DC):
                    for k, (a, b) in enumerate(((0, 0), (0, 1), (1, 0))):
                        for n in range(2):
                            mm = nc.tensor.matmul(out_ps[:, n * 512:(n + 1) * 512], x[a][:, c, :],
                                                  (w_hi, w_lo)[b][:, l, c, n * 512:(n + 1) * 512],
                                                  start=(c == 0 and k == 0), stop=(c == DC - 1 and k == 2))
                mm.then_inc(done, 1)

            def last_layer(t):
                pe.wait_ge(x_lo_done, t + 1)
                pe.wait_ge(out_done, t + ONE)
                product(f_ps, (x_hi, x_lo), 1, f_ready)

            def tile(t, s, first, last):
                pe.wait_ge(a_lo_done, t + 1)
                if not first:
                    pe.wait_ge(h1_done, t)
                product(o_ps, (a_hi, a_lo), 0, o_ready)
                if not first:
                    last_layer(t - 1)
                turn_x(t, first)

            tiles(pe, tile)
            last_layer(TILES - 1)


def build(nc, x_ctx, t0, t1, t2, t3, tok_b, w_qkv_t, b_qk, b_v, w_o_t, b_o, w_base_t, b_base, enc, coefs, mask,
          rope, fourier_t, ident, mask_qk, mask_kq, out):
    scratch = lambda n, s, d: nc.dram_tensor(n, s, d, kind="Internal").ap()
    h_dram = scratch("h_scratch", [TOKENS, D], F32)
    q_hi = scratch("q_hi_scratch", [BATCH * Q_DIM, SEQ], F32)
    q_lo = scratch("q_lo_scratch", [BATCH * Q_DIM, SEQ], F32)
    k_hi = scratch("k_hi_scratch", [BATCH * KV_DIM, SEQ], F32)
    k_lo = scratch("k_lo_scratch", [BATCH * KV_DIM, SEQ], F32)
    v_dram = scratch("v_scratch", [GROUPS, P, QT, VW], F32)
    o_hi_dram = scratch("o_hi_scratch", [BATCH * Q_DIM, SEQ], F32)
    o_lo_dram = scratch("o_lo_scratch", [BATCH * Q_DIM, SEQ], F32)
    den_dram = scratch("den_scratch", [BATCH * Q_DIM, SEQ], F32)
    part_a(nc, x_ctx, (t0, t1, t2, t3), tok_b, w_qkv_t, b_qk, b_v, rope, h_dram, q_hi, q_lo, k_hi, k_lo, v_dram, ident)
    part_b(nc, q_hi, q_lo, k_hi, k_lo, v_dram, o_hi_dram, o_lo_dram, den_dram, ident, mask_qk, mask_kq)
    part_c(nc, o_hi_dram, o_lo_dram, den_dram, h_dram, w_o_t, b_o, w_base_t, b_base, enc, coefs, mask, fourier_t,
           ident, out)


def rope_table():
    inv = (1.0 / np.float32(10000.0) ** (np.arange(0, HD, 2, dtype=np.float32) / np.float32(HD))).astype(np.float32)
    ang = np.arange(SEQ, dtype=np.float32)[:, None] * inv[None, :]
    cos, sin = np.cos(ang).T, np.sin(ang).T
    cos = np.repeat(cos, 2, axis=0)
    sin = np.stack([-sin, sin], axis=1).reshape(HD, SEQ)
    tab = np.tile(np.stack([cos, sin], axis=1), (P // HD, 1, 1))
    tab = tab.reshape(P, 2, QC, CT).transpose(2, 0, 1, 3)
    return np.ascontiguousarray(np.concatenate([tab] * BATCH)).astype(np.float32)


def fourier_matrix_t():
    n = D
    o = np.arange(n)
    rows = np.zeros((n, n))
    rows[0] = 1.0 / np.sqrt(n)
    f = np.arange(1, (n - 1) // 2 + 1)
    ang = 2.0 * np.pi * ((f[:, None] * o[None, :]) % n) / n
    rows[1:2 * len(f):2] = np.sqrt(2.0 / n) * np.cos(ang)
    rows[2:2 * len(f) + 1:2] = np.sqrt(2.0 / n) * np.sin(ang)
    rows[n - 1] = np.where(o % 2 == 0, 1.0, -1.0) / np.sqrt(n)
    return rows.astype(np.float32)


def kernel(**inputs):
    import concourse.bacc as _bacc
    from concourse.bass_utils import run_bass_kernel_spmd as _run

    a = {k: np.asarray(v) for k, v in inputs.items()}
    x = a["x"]
    ctx = [np.concatenate([np.full((BATCH, s), VOCAB, x.dtype), x[:, :SEQ - s]], axis=1) for s in (3, 2, 1, 0)]
    ctx = np.stack(ctx, axis=-1).reshape(CHUNKS, TPC, P, ORDER).transpose(2, 0, 1, 3).reshape(P, CHUNKS, TPC * ORDER)
    tok = a["L0_tok_W"].T.reshape(ORDER, VOCAB + 1, VOCAB)
    b_qkv = a["L0_attn_b_qkv"]
    order = np.arange(P)
    arrays = {"x_ctx": ctx}
    arrays.update({f"tok_table{k}": tok[k] for k in range(ORDER)})
    arrays.update({
        "tok_b": a["L0_tok_b"],
        "w_qkv_t": a["L0_attn_w_qkv"].T,
        "b_qk": b_qkv[:Q_DIM + KV_DIM].reshape(QK_TILES, P).T,
        "b_v": b_qkv[Q_DIM + KV_DIM:],
        "w_o_t": a["L0_attn_w_o"].T,
        "b_o": a["L0_attn_b_o"],
        "w_base_t": a["L0_ffn_W_base"].T,
        "b_base": a["L0_ffn_b_base"],
        "enc": np.concatenate([a["L0_ffn_enc0"], a["L0_ffn_enc1"]], axis=0),
        "coefs": np.concatenate([a["L0_ffn_coefs0"], a["L0_ffn_coefs1"]], axis=2),
        "mask": np.concatenate([a["L0_ffn_mask0"], a["L0_ffn_mask1"]], axis=2),
        "rope": rope_table(),
        "fourier_t": fourier_matrix_t(),
        "ident": np.eye(P, dtype=np.float32),
        "mask_qk": np.where(order[None, :] > order[:, None], MASKED, 0.0).astype(np.float32),
        "mask_kq": np.where(order[None, :] < order[:, None], MASKED, 0.0).astype(np.float32),
    })
    nc = _bacc.Bacc("TRN2", target_bir_lowering=False, num_devices=1)
    maps, args = {}, []
    for name, value in arrays.items():
        value = np.ascontiguousarray(value)
        maps[f"in_{name}"] = value
        args.append(nc.dram_tensor(f"in_{name}", value.shape, mybir.dt.from_np(value.dtype), kind="ExternalInput").ap())
    args.append(nc.dram_tensor("out_dram", (TOKENS, D), F32, kind="ExternalOutput").ap())
    build(nc, *args)
    r = _run(nc, [maps], core_ids=[0])
    return r.results[0]["out_dram"].reshape(BATCH, SEQ, D)
```

```python
from contextlib import ExitStack

import numpy as np

import concourse.bass as bass
from concourse import mybir

P = 128
F32 = mybir.dt.float32
F32R = mybir.dt.float32r
I32 = mybir.dt.int32
U8 = mybir.dt.uint8
ALU = mybir.AluOpType
ACT = mybir.ActivationFunctionType
AX = mybir.AxisListType.X

BATCH, SEQ, D, VOCAB, ORDER = 2, 2048, 1024, 1024, 4
HEADS, KV_HEADS, HD = 32, 8, 32
GROUP = HEADS // KV_HEADS
Q_DIM, KV_DIM = HEADS * HD, KV_HEADS * HD
QKV_DIM = Q_DIM + 2 * KV_DIM
EPS = 1e-5
R0, R1, E = 32, 8, 3
R = R0 + R1
SCALING = 16.0 / 32.0
DC = D // P
TOKENS = BATCH * SEQ
CT = 512
CHUNKS = TOKENS // CT
TPC = CT // P
QK_TILES = (Q_DIM + KV_DIM) // P
Q_TILES = Q_DIM // P
TILES = TOKENS // P
W_SLOTS = 4
V_SLOTS = 4
NORM_BEHIND = (3, 5, 7, 8)
VW = 3 * HD
QT = SEQ // P
QC = SEQ // CT
ALL_HEADS = BATCH * HEADS
GROUPS = ALL_HEADS // GROUP
MASKED = -1e30
K_ROWS, M_ROW = 96, 96


class Steps:

    def __init__(self, eng, sem, base):
        self.eng, self.sem, self.at = eng, sem, base

    def do(self, ins):
        self.at = self.at + 1
        ins.then_inc(self.sem, 1)
        self.eng.wait_ge(self.sem, self.at)


def pass_waits(eng, passed):
    eng.sem_inc(passed, 1)


def part_a(nc, x_ctx, tables, tok_b, w_qkv_t, b_qk, b_v, rope, h_dram, q_hi, q_lo, k_hi, k_lo, v_dram, ident_in):
    with ExitStack() as ctx:
        sb = lambda n, s, d: ctx.enter_context(nc.sbuf_tensor(n, s, d))
        sem = lambda n: ctx.enter_context(nc.semaphore(n))
        w_hi = sb("w_hi", [P, DC, QKV_DIM], F32R)
        w_lo = sb("w_lo", [P, DC, QKV_DIM], F32R)
        x_hi = sb("x_hi", [P, DC, CT], F32R)
        x_lo = sb("x_lo", [P, DC, CT], F32R)
        hbuf = sb("hbuf", [P, TPC, D], F32)
        xn = sb("xn", [P, TPC, D], F32)
        tab = sb("tab", [P, 2, CT], F32)
        rotation = sb("rotation", [P, 6, CT], F32)
        qf, qsw, qrot = (rotation[:, 2 * k:2 * k + 2, :] for k in range(3))
        rot_hi = sb("rot_hi", [P, 2, CT], F32R)
        rot_lo = sb("rot_lo", [P, 2, CT], F32R)
        vf = sb("vf", [P, 2, KV_DIM], F32)
        vt = sb("vt", [P, V_SLOTS, KV_HEADS, VW], F32R)
        tokb = sb("tokb", [P, D], F32)
        bqk = sb("bqk", [P, QK_TILES], F32)
        bv = sb("bv", [P, KV_DIM], F32)
        ident = sb("ident", [P, P], F32)
        idx_all = sb("idx_all", [P, CHUNKS, TPC * ORDER], I32)
        idx = sb("idx", [P, TPC * ORDER], I32)
        stats = sb("stats", [P, 2, 6], F32)
        mv = sb("mv", [P, 2], F32)
        var = sb("var", [P, 1], F32)
        std = sb("std", [P, 1], F32)
        rstd = sb("rstd", [P, 2], F32)
        shift = sb("shift", [P, 2], F32)
        w_in = [buf[:, s * QKV_DIM:(s + 1) * QKV_DIM]
                for buf in (xn[:].rearrange("p t d -> p (t d)"), rotation[:].rearrange("p s t -> p (s t)"))
                for s in range(W_SLOTS // 2)]
        tr_ps = ctx.enter_context(nc.psum_tensor("tr_ps", [P, 2, DC, P], F32))
        qk_ps = ctx.enter_context(nc.psum_tensor("qk_ps", [P, 2, CT], F32))
        v_ps = ctx.enter_context(nc.psum_tensor("v_ps", [P, 2, 512], F32))

        consts = sem("consts")
        w_loaded = [sem(f"w_loaded{s}") for s in range(W_SLOTS)]
        w_hi_done, w_lo_done = sem("w_hi_done"), sem("w_lo_done")
        idx_loaded, idx_copied = sem("idx_loaded"), sem("idx_copied")
        gathered = [sem(f"gathered{t}") for t in range(TPC)]
        h_ready, h_stored = sem("h_ready"), sem("h_stored")
        ln_step, var_ready, std_ready = sem("ln_step"), sem("var_ready"), sem("std_ready")
        norm_ready, xn_ready, tr_ready = sem("norm_ready"), sem("xn_ready"), sem("tr_ready")
        x_hi_done, x_lo_done = sem("x_hi_done"), sem("x_lo_done")
        qk_ready, qf_done = sem("qk_ready"), sem("qf_done")
        rot_step, rot_done = sem("rot_step"), sem("rot_done")
        rhi_done, rlo_done = sem("rhi_done"), sem("rlo_done")
        rot_stored = [sem(f"rot_stored{s}") for s in range(2)]
        tab_loaded, ones_set = sem("tab_loaded"), sem("ones_set")
        dve_passed, pool_passed = sem("dve_passed"), sem("pool_passed")
        v_ready, v_done = sem("v_ready"), sem("v_done")
        v_hi_done, v_lo_done = sem("v_hi_done"), sem("v_lo_done")
        v_stored = [sem(f"v_stored{s}") for s in range(V_SLOTS)]
        EMPTY = 16
        AHEAD = 2
        block = ctx.enter_context(nc.Block())

        @block.sync
        def _(sp):
            sp.dma_start(idx_all[:], x_ctx).then_inc(idx_loaded, 16)
            sp.dma_start(ident[:], ident_in).then_inc(consts, 16)
            sp.dma_start(tokb[:], tok_b.rearrange("(a d) -> a d", a=1).broadcast_to([P, D])).then_inc(consts, 16)
            sp.dma_start(bqk[:], b_qk).then_inc(consts, 16)
            sp.dma_start(bv[:], b_v.rearrange("(a d) -> a d", a=1).broadcast_to([P, KV_DIM])).then_inc(consts, 16)
            for c in range(DC):
                if c >= W_SLOTS:
                    sp.wait_ge(w_lo_done, c - W_SLOTS + 1)
                sp.dma_start(w_in[c % W_SLOTS], w_qkv_t[c * P:(c + 1) * P, :]).then_inc(w_loaded[c % W_SLOTS], 16)
            sp.dma_start(tab[:], rope[0]).then_inc(tab_loaded, 16)

            def store_h(m, t):
                sp.wait_ge(h_ready, m * TPC + t + 1)
                sp.dma_start(h_dram[bass.ds(m * CT + t * P, P), :], hbuf[:, t, :]).then_inc(h_stored, 16)

            def store_rotated(n, f):
                sp.wait_ge(rlo_done, n * QK_TILES + f + 1)
                hi, lo, row = (q_hi, q_lo, f * P) if f < Q_TILES else (k_hi, k_lo, (f - Q_TILES) * P)
                at = (slice(None), bass.ds((n % QC) * CT, CT))
                for dst, src in ((hi, rot_hi), (lo, rot_lo)):
                    dst_rows = dst[bass.ds((n // QC) * (Q_DIM if f < Q_TILES else KV_DIM) + row, P), :]
                    sp.dma_start(dst_rows[at], src[:, f % 2, :].bitcast(F32)).then_inc(rot_stored[f % 2], 16)

            def chunk(n, last):
                for f in range(QK_TILES):
                    if not last and f in NORM_BEHIND:
                        store_h(n + 1, NORM_BEHIND.index(f))
                    store_rotated(n, f)
                if not last:
                    sp.wait_ge(rot_done, (n + 1) * QK_TILES + AHEAD)
                    sp.dma_start(tab[:], rope[n + 1]).then_inc(tab_loaded, 16)
                for t in range(TPC):
                    sp.wait_ge(v_lo_done, n * TPC + t + 1 + AHEAD)
                    to = v_dram[bass.ds((n // QC) * KV_HEADS, KV_HEADS), :, bass.ds((n % QC) * TPC + t, 1), :]
                    sp.dma_start(to.rearrange("g p a w -> p g (a w)"),
                                 vt[:, t, :, :].bitcast(F32)).then_inc(v_stored[t], 16)

            for t in range(TPC):
                store_h(0, t)
            with sp.Fori(0, CHUNKS - 1) as n:
                chunk(n, False)
            chunk(CHUNKS - 1, True)
            sp.wait_ge(h_stored, 16 * TILES)
            for s in range(2):
                sp.wait_ge(rot_stored[s], EMPTY + 16 * CHUNKS * QK_TILES)
            for s in range(V_SLOTS):
                sp.wait_ge(v_stored[s], EMPTY + 16 * CHUNKS * TPC // V_SLOTS)

        @block.gpsimd
        def _(pool):
            pool.wait_ge(idx_loaded, 16)

            def gather(m, first):
                nc.gpsimd.tensor_copy(idx[:], idx_all[:, m, :] if first else
                                      idx_all[:, bass.ds(m, 1), :].rearrange("p a k -> p (a k)")
                                      ).then_inc(idx_copied, 1)
                pool.wait_ge(idx_copied, m + 1)
                if not first:
                    pool.wait_ge(h_stored, 16 * TPC * m)
                for k in range(ORDER):
                    for t in range(TPC):
                        if k == 0 and not first:
                            pool.wait_ge(xn_ready, m * TPC - TPC + t + 1)
                        if k > 0:
                            pool.wait_ge(gathered[t], 16 * (m * ORDER + k))
                        pass_waits(pool, pool_passed)
                        j = t * ORDER + k
                        nc.gpsimd.indirect_dma_start(
                            hbuf[:, t, :], None, tables[k],
                            bass.IndirectOffsetOnAxis(ap=idx[:, j:j + 1], axis=0),
                            compute_op=ALU.bypass if k == 0 else ALU.add).then_inc(gathered[t], 16)
                for t in range(TPC):
                    pool.wait_ge(gathered[t], 16 * (m + 1) * ORDER)

            gather(0, True)
            with pool.Fori(1, CHUNKS) as m:
                gather(m, False)

        @block.scalar
        def _(act):
            act.sem_inc(qf_done, AHEAD)
            for s in range(2):
                act.sem_inc(rot_stored[s], EMPTY)
            for s in range(V_SLOTS):
                act.sem_inc(v_stored[s], EMPTY)
            for c in range(DC):
                act.wait_ge(w_loaded[c % W_SLOTS], 16 * (c // W_SLOTS + 1))
                nc.scalar.copy(w_hi[:, c, :], w_in[c % W_SLOTS]).then_inc(w_hi_done, 1)
            act.wait_ge(consts, 64)

            def deviation(m, t):
                act.wait_ge(var_ready, m * TPC + t + 1)
                nc.scalar.activation(std[:], var[:], ACT.Sqrt).then_inc(std_ready, 1)

            def normalise(m, t):
                act.wait_ge(norm_ready, m * TPC + t + 1)
                if not (isinstance(m, int) and m == 0):
                    act.wait_ge(tr_ready, m * TPC - TPC + t + 1)
                nc.scalar.activation(xn[:, t, :], hbuf[:, t, :], ACT.Identity, scale=rstd[:, t % 2:t % 2 + 1],
                                     bias=shift[:, t % 2:t % 2 + 1]).then_inc(xn_ready, 1)

            def x_high(m, t):
                if not (isinstance(m, int) and m == 0):
                    act.wait_ge(v_ready, m * TPC - TPC + t + 1)
                act.wait_ge(tr_ready, m * TPC + t + 1)
                nc.scalar.copy(x_hi[:, :, t * P:(t + 1) * P], tr_ps[:, t % 2]).then_inc(x_hi_done, 1)

            def add_bias(n, f):
                act.wait_ge(qk_ready, n * QK_TILES + f + 1)
                act.wait_ge(rot_done, n * QK_TILES + f + 1)
                nc.scalar.activation(qf[:, f % 2, :], qk_ps[:, f % 2, :], ACT.Identity,
                                     bias=bqk[:, f:f + 1]).then_inc(qf_done, 1)

            def rot_high(n, f):
                act.wait_ge(rot_done, n * QK_TILES + f + 1 + AHEAD)
                act.wait_ge(rot_stored[f % 2], EMPTY + 32 * (n * (QK_TILES // 2) + f // 2))
                nc.scalar.copy(rot_hi[:, f % 2, :], qrot[:, f % 2, :]).then_inc(rhi_done, 1)

            def v_high(n, t):
                act.wait_ge(v_done, n * TPC + t + 1 + AHEAD)
                act.wait_ge(v_stored[t], EMPTY + 16 * n)
                nc.scalar.copy(vt[:, t, :, 0:HD], vf[:, t % 2, :].rearrange("p (h w) -> p h w", w=HD)
                               ).then_inc(v_hi_done, 1)

            def chunk(n, last):
                for f in range(QK_TILES):
                    add_bias(n, f)
                    if f >= 1:
                        rot_high(n, f - 1)
                    if not last and f - 1 in NORM_BEHIND:
                        normalise(n + 1, NORM_BEHIND.index(f - 1))
                    if not last and f in NORM_BEHIND:
                        deviation(n + 1, NORM_BEHIND.index(f))
                for t in range(TPC):
                    if not last:
                        x_high(n + 1, t)
                    if t == 0:
                        rot_high(n, QK_TILES - 1)
                    v_high(n, t)

            for t in range(TPC):
                deviation(0, t)
                normalise(0, t)
            for t in range(TPC):
                x_high(0, t)
            with act.Fori(0, CHUNKS - 1) as n:
                chunk(n, False)
            chunk(CHUNKS - 1, True)

        @block.vector
        def _(dve):
            dve.sem_inc(rot_done, AHEAD)
            dve.sem_inc(v_done, AHEAD)
            dve.sem_inc(v_lo_done, AHEAD)
            nc.vector.memset(vt[:].bitcast(F32), 1.0).then_inc(ones_set, 1)
            for c in range(DC):
                dve.wait_ge(w_hi_done, c + 1)
                nc.vector.tensor_tensor(w_lo[:, c, :], w_in[c % W_SLOTS], w_hi[:, c, :].bitcast(F32),
                                        ALU.subtract).then_inc(w_lo_done, 1)
            dve.wait_ge(ones_set, 1)
            dve.wait_ge(consts, 64)
            LN_STEPS, ROT_STEPS = 4, 3

            def layer_norm(m, t):
                at = m * TPC + t
                step = Steps(dve, ln_step, at * LN_STEPS)
                h = hbuf[:, t, :]
                dve.wait_ge(gathered[t], 16 * ORDER * (m + 1))
                nc.vector.tensor_tensor(h, h, tokb[:], ALU.add).then_inc(h_ready, 1)
                dve.wait_ge(h_ready, at + 1)
                step.do(nc.vector.bn_stats(stats[:, 0, :], h[:, 0:512]))
                step.do(nc.vector.bn_stats(stats[:, 1, :], h[:, 512:1024]))
                pass_waits(dve, dve_passed)
                step.do(nc.vector.bn_aggr(mv[:], stats[:].rearrange("p a s -> p (a s)")))
                nc.vector.tensor_scalar(var[:], mv[:, 1:2], EPS, None, ALU.add).then_inc(var_ready, 1)
                dve.wait_ge(std_ready, at + 1)
                if not (isinstance(m, int) and m == 0 and t < 2):
                    dve.wait_ge(xn_ready, at - 1)
                step.do(nc.vector.reciprocal(rstd[:, t % 2:t % 2 + 1], std[:]))
                nc.vector.tensor_scalar(shift[:, t % 2:t % 2 + 1], mv[:, 0:1], rstd[:, t % 2:t % 2 + 1], -1.0,
                                               ALU.mult, ALU.mult).then_inc(norm_ready, 1)
                dve.wait_ge(norm_ready, at + 1)

            def x_low(m, t):
                dve.wait_ge(x_hi_done, m * TPC + t + 1)
                sl = slice(t * P, (t + 1) * P)
                nc.vector.tensor_tensor(x_lo[:, :, sl], tr_ps[:, t % 2], x_hi[:, :, sl].bitcast(F32),
                                        ALU.subtract).then_inc(x_lo_done, 1)

            swap = [i ^ 1 for i in range(32)]

            def rotate(n, f):
                at = n * QK_TILES + f
                step = Steps(dve, rot_step, at * ROT_STEPS)
                s = f % 2
                dve.wait_ge(qf_done, at + 1 + AHEAD)
                if f == 0:
                    dve.wait_ge(tab_loaded, 16 * (n + 1))
                pass_waits(dve, dve_passed)
                step.do(nc.vector.stream_shuffle(qsw[:, s, :], qf[:, s, :], swap))
                step.do(nc.vector.tensor_tensor(qsw[:, s, :], qsw[:, s, :], tab[:, 1, :], ALU.mult))
                step.do(nc.vector.tensor_tensor(qrot[:, s, :], qf[:, s, :], tab[:, 0, :], ALU.mult))
                nc.vector.tensor_tensor(qrot[:, s, :], qrot[:, s, :], qsw[:, s, :], ALU.add).then_inc(rot_done, 1)

            def rot_low(n, f):
                dve.wait_ge(rhi_done, n * QK_TILES + f + 1)
                nc.vector.tensor_tensor(rot_lo[:, f % 2, :], qrot[:, f % 2, :], rot_hi[:, f % 2, :].bitcast(F32),
                                        ALU.subtract).then_inc(rlo_done, 1)

            def values(n, t):
                dve.wait_ge(v_ready, n * TPC + t + 1)
                dve.wait_ge(v_lo_done, n * TPC + t + 1)
                nc.vector.tensor_tensor(vf[:, t % 2, :], v_ps[:, t % 2, 0:KV_DIM], bv[:], ALU.add
                                        ).then_inc(v_done, 1)

            def v_low(n, t):
                dve.wait_ge(v_hi_done, n * TPC + t + 1)
                nc.vector.tensor_tensor(vt[:, t, :, HD:2 * HD], vf[:, t % 2, :].rearrange("p (h w) -> p h w", w=HD),
                                        vt[:, t, :, 0:HD].bitcast(F32), ALU.subtract).then_inc(v_lo_done, 1)

            def chunk(n, last):
                for f in range(QK_TILES):
                    rotate(n, f)
                    if f >= 1:
                        rot_low(n, f - 1)
                    if f in NORM_BEHIND and not last:
                        layer_norm(n + 1, NORM_BEHIND.index(f))
                for t in range(TPC):
                    values(n, t)
                    if not last:
                        x_low(n + 1, t)
                    if t == 0:
                        rot_low(n, QK_TILES - 1)
                    else:
                        v_low(n, t - 1)
                v_low(n, TPC - 1)

            for t in range(TPC):
                layer_norm(0, t)
            for t in range(TPC):
                x_low(0, t)
            with dve.Fori(0, CHUNKS - 1) as n:
                chunk(n, False)
            chunk(CHUNKS - 1, True)

        @block.tensor
        def _(pe):
            pe.wait_ge(consts, 64)
            pe.wait_ge(w_lo_done, DC)

            def transpose(m, t):
                at = m * TPC + t
                pe.wait_ge(xn_ready, at + 1)
                if not (isinstance(m, int) and m == 0 and t < 2):
                    pe.wait_ge(x_lo_done, at - 1)
                for c in range(DC):
                    mm = nc.tensor.transpose(tr_ps[:, t % 2, c, :], xn[:, t, c * P:(c + 1) * P], ident[:])
                mm.then_inc(tr_ready, 1)

            def chunk(n, last):
                pe.wait_ge(x_lo_done, (n + 1) * TPC)
                for f in range(QK_TILES):
                    pe.wait_ge(qf_done, n * QK_TILES + f + 1)
                    for c in range(DC):
                        w = (w_hi[:, c, f * P:(f + 1) * P], w_lo[:, c, f * P:(f + 1) * P])
                        x = (x_hi[:, c, :], x_lo[:, c, :])
                        for k, (a, b) in enumerate(((0, 0), (0, 1), (1, 0))):
                            mm = nc.tensor.matmul(qk_ps[:, f % 2, :], w[a], x[b], start=(c == 0 and k == 0),
                                                  stop=(c == DC - 1 and k == 2))
                    mm.then_inc(qk_ready, 1)
                if not last:
                    transpose(n + 1, 0)
                    transpose(n + 1, 1)
                for t in range(TPC):
                    pe.wait_ge(v_done, n * TPC + t + 1)
                    for c in range(DC):
                        w = (w_hi[:, c, Q_DIM + KV_DIM:], w_lo[:, c, Q_DIM + KV_DIM:])
                        x = (x_hi[:, c, t * P:(t + 1) * P], x_lo[:, c, t * P:(t + 1) * P])
                        for k, (a, b) in enumerate(((0, 0), (1, 0), (0, 1))):
                            mm = nc.tensor.matmul(v_ps[:, t % 2, 0:KV_DIM], x[b], w[a], start=(c == 0 and k == 0),
                                                  stop=(c == DC - 1 and k == 2))
                    mm.then_inc(v_ready, 1)
                    if not last and 0 < t < TPC - 1:
                        transpose(n + 1, t + 1)

            for t in range(TPC):
                transpose(0, t)
            with pe.Fori(0, CHUNKS - 1) as n:
                chunk(n, False)
            chunk(CHUNKS - 1, True)


def score_units():
    return [(c, kt, max(0, kt - c * TPC)) for c in range(QC) for kt in range(TPC * (c + 1))]


def max_units():
    return [(i, j, CT if j < i // TPC else (i % TPC + 1) * P) for i in range(QT) for j in range(i // TPC + 1)]


UNITS, MAXES = score_units(), max_units()
NU, NM = len(UNITS), len(MAXES)
LAST_OF = [max(u for u, (c, _, _) in enumerate(UNITS) if c == k) for k in range(QC)]
HIGH, LOW, LAG = 2, 5, 9
TURN = 34
SLOTS = 10
SCORE_BANKS, MAX_BANKS = 2, 4
HIGH_DVE = [2, 8, 9, 12, 13, 15, 19, 20, 27, 28, 31, 32]
LOW_DVE = [0, 2, 3, 19, 20, 32, 33, 34, 36, 38]
LOW_POOL = [u for u in range(NU) if u not in LOW_DVE]
MAXES_IN = [1, 0, 2, 0, 0, 2, 1, 2, 2, 0, 1, 0, 1, 1, 1, 0, 1, 1, 2, 1,
            1, 2, 0, 0, 0, 3, 1, 0, 1, 2, 2, 1, 0, 0, 3, 0, 1, 0, 1, 3]
MAXES_AFTER = [sum(MAXES_IN[TURN:]) + sum(MAXES_IN[:u + 1]) if u < TURN else sum(MAXES_IN[TURN:u + 1])
               for u in range(NU)]
EARLY = MAXES_AFTER[NU - 1]


def head_plan(first, more, two_more):
    plan, n = [], EARLY
    for u in range(NU if more else NU + LAG):
        if u < NU:
            plan.append(("score", u, 0))
        if u == TURN + 2 and more:
            plan.append(("rows", 0, 0))
        for what, lag in (("high", HIGH), ("low", LOW)):
            if 0 <= u - lag < NU:
                plan.append((what, u - lag, 0))
            elif u < lag and not first:
                plan.append((what, NU + u - lag, 1))
        if u == TURN:
            n = 0
        while u < NU and n < MAXES_AFTER[u]:
            if two_more if u >= TURN else more:
                plan.append(("max", n, -2 if u >= TURN else -1))
            n += 1
            if n == NM and more:
                plan.append(("all_max", 0, 0))
        if u >= LAG:
            plan.append(("value", u - LAG, 0))
        elif not first:
            plan.append(("value", NU + u - LAG, 1))
        if u == TURN and more:
            plan.append(("turn", 0, 0))
    return plan


def part_b(nc, q_hi, q_lo, k_hi, k_lo, v_dram, o_hi_dram, o_lo_dram, den_dram, ident_in, mask_qk, mask_kq):
    with ExitStack() as ctx:
        sb = lambda n, s, d: ctx.enter_context(nc.sbuf_tensor(n, s, d))
        sem = lambda n: ctx.enter_context(nc.semaphore(n))
        qs = [sb(f"qs{s}", [P, SEQ], F32R) for s in range(GROUP)]
        ks = [sb(f"ks{s}", [P, SEQ], F32R) for s in range(2)]
        vs = [sb(f"vs{s}", [P, QT, VW], F32R) for s in range(2)]
        probs = sb("probs", [P, SLOTS, CT], F32)
        p_hi = sb("p_hi", [P, SLOTS, CT], F32R)
        p_lo = sb("p_lo", [P, SLOTS, CT], F32R)
        o_sb = sb("o_sb", [VW, 2, SEQ], F32)
        mpart = sb("mpart", [P, QT, QC], F32)
        mcol = sb("mcol", [P, QT], F32)
        m_hi = sb("m_hi", [QT, P], F32R)
        m_lo = sb("m_lo", [QT, P], F32R)
        ident = sb("ident_b", [P, P], F32)
        consts_in = sb("consts_in", [P, 3, P], F32)
        consts_r = sb("consts_r", [P, 3, P], F32R)
        identr, mqk, mkq = (consts_r[:, j, :] for j in range(3))
        st_ps = ctx.enter_context(nc.psum_tensor("st_ps", [P, SCORE_BANKS, CT], F32))
        mx_ps = ctx.enter_context(nc.psum_tensor("mx_ps", [P, MAX_BANKS, CT], F32))
        o_ps = ctx.enter_context(nc.psum_tensor("o_ps", [P, 2, CT], F32))
        mt_ps = o_ps[0:QT, 0, 0:P]

        q_loaded = [sem(f"q_loaded{s}") for s in range(GROUP)]
        kv_loaded = [sem(f"kv_loaded{s}") for s in range(2)]
        consts, consts_done, ones_done = sem("consts_b"), sem("consts_done"), sem("ones_done")
        max_ready, max_done, max_all = sem("max_ready"), sem("max_done"), sem("max_all")
        turned, m_hi_done, m_lo_done, m_rows = sem("turned"), sem("m_hi_done"), sem("m_lo_done"), sem("m_rows")
        st_ready, exp_done, hi_done = sem("st_ready"), sem("exp_done"), sem("hi_done")
        lo_dve_done, lo_pool_done = sem("lo_dve_done"), sem("lo_pool_done")
        pv_done, o_done = sem("pv_done"), sem("o_done")
        o_stored = [sem(f"o_stored{s}") for s in range(2)]
        P_FREE, O_FREE = SLOTS, 2
        EMPTY = 16
        Q_LOAD, KV_LOAD, STORE = 3 * 16, 4 * 16, 3 * 16
        block = ctx.enter_context(nc.Block())

        def kv_of(s):
            return 0 if s == 0 else 1

        def max_k_of(s):
            return 0 if s < 2 else 1

        def lo_done(h, u):
            if u in LOW_POOL:
                return lo_pool_done, h * len(LOW_POOL) + LOW_POOL.index(u) + 1
            return lo_dve_done, h * len(LOW_DVE) + LOW_DVE.index(u) + 1

        def maxima_before(eng, g, reg):
            if isinstance(g, int):
                return g * (GROUP * NM)
            eng.reg_mul(reg, g, GROUP * NM)
            return eng.snap(reg)

        def split_ready(h, u):
            if u in HIGH_DVE:
                return hi_done, h * len(HIGH_DVE) + HIGH_DVE.index(u) + 1
            return exp_done, h * NU + u + 1

        def groups(eng, group):
            group(0, True, False)
            with eng.Fori(1, GROUPS - 1) as g:
                group(g, False, False)
            group(GROUPS - 1, False, True)

        def heads(g, first, last):
            return [(g * GROUP + s, s, head_plan(first and s == 0, not (last and s == GROUP - 1),
                                                 not (last and s >= GROUP - 2))) for s in range(GROUP)]

        @block.sync
        def _(sp):
            for j, a in enumerate((ident_in, mask_qk, mask_kq)):
                sp.dma_start(consts_in[:, j, :], a).then_inc(consts, 16)
            sp.dma_start(ident[:], ident_in).then_inc(consts, 16)

            def load_q(g, s):
                row = g * (GROUP * HD) + s * HD
                for r, q in enumerate((q_hi, q_hi, q_lo)):
                    sp.dma_start(qs[s][r * HD:(r + 1) * HD, :].bitcast(F32), q[bass.ds(row, HD), :]
                                 ).then_inc(q_loaded[s], 16)

            def load_kv(g, b):
                for r, k in enumerate((k_hi, k_lo, k_hi)):
                    sp.dma_start(ks[b][r * HD:(r + 1) * HD, :].bitcast(F32), k[bass.ds(g * HD, HD), :]
                                 ).then_inc(kv_loaded[b], 16)
                sp.dma_start(vs[b][:].bitcast(F32), v_dram[bass.ds(g, 1)].rearrange("a p t w -> (a p) t w")
                             ).then_inc(kv_loaded[b], 16)

            def store(g, s):
                h = g * GROUP + s
                sp.wait_ge(o_done, O_FREE + (h + 1) * QC)
                for r, dst in enumerate((o_hi_dram, o_lo_dram)):
                    sp.dma_start(dst[bass.ds(h * HD, HD), :], o_sb[r * HD:(r + 1) * HD, s % 2, :]
                                 ).then_inc(o_stored[s % 2], 16)
                sp.dma_start(den_dram[bass.ds(h, 1), :], o_sb[2 * HD:2 * HD + 1, s % 2, :]).then_inc(o_stored[s % 2], 16)

            def send_rows(h, s):
                for r, (m, done) in enumerate(((m_hi, m_hi_done), (m_lo, m_lo_done))):
                    sp.wait_ge(done, h + 1)
                    sp.dma_start(qs[s][M_ROW + r:M_ROW + r + 1, :].bitcast(F32).rearrange("a (t p) -> a t p", p=P),
                                 m[:].bitcast(F32)).then_inc(m_rows, 16)

            def group(g, last):
                for s in range(GROUP):
                    if not (last and s == GROUP - 1):
                        send_rows(g * GROUP + s + 1, (s + 1) % GROUP)
                    store(g, s)
                    if last:
                        continue
                    sp.wait_ge(pv_done, P_FREE + (g * GROUP + s + 1) * NU)
                    load_q(g + 1, s)
                    if s == 1:
                        load_kv(g + 1, 0)
                    if s == GROUP - 1:
                        load_kv(g + 1, 1)

            load_q(0, 0)
            load_kv(0, 0)
            load_q(0, 1)
            load_kv(0, 1)
            load_q(0, 2)
            load_q(0, 3)
            send_rows(0, 0)
            with sp.Fori(0, GROUPS - 1) as g:
                group(g, False)
            group(GROUPS - 1, True)
            for s in range(2):
                sp.wait_ge(o_stored[s], EMPTY + STORE * ALL_HEADS // 2)

        @block.gpsimd
        def _(pool):
            pool.wait_ge(consts, 64)
            nc.gpsimd.tensor_copy(consts_r[:], consts_in[:]).then_inc(consts_done, 1)

            def low(h, u):
                w = CT - UNITS[u][2] * P
                pool.wait_ge(*split_ready(h, u))
                nc.gpsimd.tensor_tensor(p_lo[:, u % SLOTS, 0:w], probs[:, u % SLOTS, 0:w],
                                        p_hi[:, u % SLOTS, 0:w].bitcast(F32), ALU.subtract).then_inc(lo_pool_done, 1)

            def group(g, first, last):
                for h, s, plan in heads(g, first, last):
                    for what, u, back in plan:
                        if what == "low" and u in LOW_POOL:
                            low(h - back, u)

            groups(pool, group)

        @block.scalar
        def _(act):
            for s in range(2):
                act.sem_inc(o_stored[s], EMPTY)

            def exps(h, u):
                w = CT - UNITS[u][2] * P
                act.wait_ge(st_ready, h * NU + u + 1)
                act.wait_ge(pv_done, h * NU + u + 1)
                if u not in HIGH_DVE:
                    nc.scalar.activation(p_hi[:, u % SLOTS, 0:w], st_ps[:, u % SCORE_BANKS, 0:w], ACT.Exp,
                                         scale=float(HD) ** -0.5)
                nc.scalar.activation(probs[:, u % SLOTS, 0:w], st_ps[:, u % SCORE_BANKS, 0:w], ACT.Exp,
                                     scale=float(HD) ** -0.5).then_inc(exp_done, 1)

            def group(g, first, last):
                for h, s, plan in heads(g, first, last):
                    for what, u, back in plan:
                        if what == "score":
                            exps(h, u)

            groups(act, group)

        @block.vector
        def _(dve):
            max_count = dve.alloc_register("max_count")
            dve.sem_inc(pv_done, P_FREE)
            dve.sem_inc(o_done, O_FREE)
            for s in range(2):
                nc.vector.memset(ks[s][M_ROW:P, :].bitcast(F32), 1.0).then_inc(ones_done, 1)

            def row_max(h, before, n):
                i, j, w = MAXES[n]
                dve.wait_ge(max_ready, before + n + 1)
                if n == 0 and not (isinstance(h, int) and h == 0):
                    dve.wait_ge(max_all, h)
                nc.vector.tensor_reduce(mpart[:, i, j:j + 1], mx_ps[:, n % MAX_BANKS, 0:w], AX, ALU.max
                                        ).then_inc(max_done, 1)

            def all_max(before):
                dve.wait_ge(max_done, before + NM)
                for g in range(QC):
                    last = nc.vector.tensor_reduce(mcol[:, g * TPC:(g + 1) * TPC],
                                                   mpart[:, g * TPC:(g + 1) * TPC, 0:g + 1], AX, ALU.max)
                last.then_inc(max_all, 1)

            def maxima_rows(h):
                dve.wait_ge(turned, h + 1)
                if not (isinstance(h, int) and h == 0):
                    dve.wait_ge(m_rows, 32 * h)
                nc.vector.tensor_scalar(m_hi[:], mt_ps, -1.0, None, ALU.mult).then_inc(m_hi_done, 1)
                dve.wait_ge(m_hi_done, h + 1)
                nc.vector.scalar_tensor_tensor(m_lo[:], mt_ps, -1.0, m_hi[:].bitcast(F32),
                                               ALU.mult, ALU.subtract).then_inc(m_lo_done, 1)

            def high(h, u):
                w = CT - UNITS[u][2] * P
                dve.wait_ge(exp_done, h * NU + u + 1)
                nc.vector.tensor_copy(p_hi[:, u % SLOTS, 0:w], probs[:, u % SLOTS, 0:w]).then_inc(hi_done, 1)

            def low(h, u):
                w = CT - UNITS[u][2] * P
                dve.wait_ge(*split_ready(h, u))
                nc.vector.tensor_tensor(p_lo[:, u % SLOTS, 0:w], probs[:, u % SLOTS, 0:w],
                                        p_hi[:, u % SLOTS, 0:w].bitcast(F32), ALU.subtract).then_inc(lo_dve_done, 1)

            def take(h, c, slot, stores_before):
                dve.wait_ge(pv_done, P_FREE + h * NU + LAST_OF[c] + 1)
                if c == 0:
                    dve.wait_ge(o_stored[slot], EMPTY + STORE * stores_before)
                nc.vector.tensor_copy(o_sb[:, slot, c * CT:(c + 1) * CT], o_ps[0:VW, c % 2, :]).then_inc(o_done, 1)

            def group(g, first, last):
                before_group = maxima_before(dve, g, max_count)
                for h, s, plan in heads(g, first, last):
                    for what, u, back in plan:
                        if what == "max":
                            row_max(h - back, before_group + (s - back) * NM, u)
                        if what == "all_max":
                            all_max(before_group + (s + 1) * NM)
                        if what == "rows":
                            maxima_rows(h + 1)
                        if what == "high" and u in HIGH_DVE:
                            high(h - back, u)
                        if what == "low" and u in LOW_DVE:
                            low(h - back, u)
                        if what == "value" and u in LAST_OF:
                            at = s - back
                            take(h - back, LAST_OF.index(u), at % 2, g * (GROUP // 2) + (at - at % 2) // 2)

            for n in range(NM):
                row_max(0, 0, n)
            all_max(0)
            for n in range(EARLY):
                row_max(1, NM, n)
            maxima_rows(0)
            groups(dve, group)

        @block.tensor
        def _(pe):
            max_count = pe.alloc_register("max_count")
            pe.wait_ge(consts_done, 1)
            pe.wait_ge(ones_done, 2)

            def row_scores(g, h, s, before, n):
                i, j, w = MAXES[n]
                if n == 0:
                    pe.wait_ge(q_loaded[s], Q_LOAD * (g + 1))
                    if s == 0:
                        pe.wait_ge(kv_loaded[0], KV_LOAD * (g + 1))
                    if s == 2:
                        pe.wait_ge(kv_loaded[1], KV_LOAD * (g + 1))
                if not (isinstance(h, int) and h == 0 and n < MAX_BANKS):
                    pe.wait_ge(max_done, before + (n - (MAX_BANKS - 1)))
                diagonal = j == i // TPC
                out = mx_ps[:, n % MAX_BANKS, 0:w]
                mm = nc.tensor.matmul(out, qs[s][0:K_ROWS, i * P:(i + 1) * P],
                                      ks[max_k_of(s)][0:K_ROWS, j * CT:j * CT + w], start=True, stop=not diagonal)
                if diagonal:
                    mm = nc.tensor.matmul(out[:, w - P:w], identr, mqk, start=False, stop=True)
                mm.then_inc(max_ready, 1)

            def turn(h):
                pe.wait_ge(max_all, h + 1)
                if not (isinstance(h, int) and h == 0):
                    pe.wait_ge(o_done, O_FREE + (h - 1) * QC + QC - 1)
                nc.tensor.transpose(mt_ps, mcol[:], ident[:]).then_inc(turned, 1)

            def scores(g, h, s, u):
                c, kt, j = UNITS[u]
                w = CT - j * P
                if u == 0:
                    pe.wait_ge(m_rows, 32 * (h + 1))
                    if s == 1:
                        pe.wait_ge(kv_loaded[1], KV_LOAD * (g + 1))
                if not (isinstance(h, int) and h == 0 and u < SCORE_BANKS):
                    pe.wait_ge(exp_done, h * NU + u - (SCORE_BANKS - 1))
                diagonal = kt >= c * TPC
                mm = nc.tensor.matmul(st_ps[:, u % SCORE_BANKS, 0:w], ks[kv_of(s)][0:M_ROW + 2, kt * P:(kt + 1) * P],
                                      qs[s][0:M_ROW + 2, c * CT + j * P:(c + 1) * CT], start=True, stop=not diagonal)
                if diagonal:
                    mm = nc.tensor.matmul(st_ps[:, u % SCORE_BANKS, 0:P], identr, mkq, start=False, stop=True)
                mm.then_inc(st_ready, 1)

            def values(h, s, u):
                c, kt, j = UNITS[u]
                w = CT - j * P
                out = o_ps[0:VW, c % 2, j * P:CT]
                pe.wait_ge(*lo_done(h, u))
                if kt == 0:
                    pe.wait_ge(o_done, h * QC + c + 1)
                v = vs[kv_of(s)][:, kt, :]
                nc.tensor.matmul(out, v, p_hi[:, u % SLOTS, 0:w], start=(kt == 0), stop=False)
                nc.tensor.matmul(out, v, p_lo[:, u % SLOTS, 0:w], start=False,
                                 stop=(u in LAST_OF)).then_inc(pv_done, 1)

            def group(g, first, last):
                before_group = maxima_before(pe, g, max_count)
                for h, s, plan in heads(g, first, last):
                    for what, u, back in plan:
                        if what == "score":
                            scores(g, h, s, u)
                        if what == "value":
                            values(h - back, (s - back) % GROUP, u)
                        if what == "max":
                            at = s - back
                            row_scores(g + at // GROUP, h - back, at % GROUP, before_group + at * NM, u)
                        if what == "turn":
                            turn(h + 1)

            for n in range(NM):
                row_scores(0, 0, 0, 0, n)
            turn(0)
            for n in range(EARLY):
                row_scores(0, 1, 1, NM, n)
            groups(pe, group)


def part_c(nc, o_hi_dram, o_lo_dram, den_dram, recip_dram, h_dram, w_o_t, b_o, w_base_t, b_base, enc, coefs, mask,
           fourier_t, ident_in, out):
    with ExitStack() as ctx:
        sb = lambda n, s, d: ctx.enter_context(nc.sbuf_tensor(n, s, d))
        sem = lambda n: ctx.enter_context(nc.semaphore(n))
        w_hi = sb("wc_hi", [P, 2, DC, D], F32R)
        w_lo = sb("wc_lo", [P, 2, DC, D], F32R)
        o_in = sb("o_in", [P, 2, 3, DC, P], F32)
        a_f = sb("a_f", [P, DC, P], F32)
        h_in = sb("h_in", [P, 2, D], F32)
        h1 = sb("h1", [P, 2, D], F32)
        xn = sb("xn_c", [P, D], F32)
        a_hi, a_lo = sb("a_hi", [P, DC, P], F32R), sb("a_lo", [P, DC, P], F32R)
        x_hi, x_lo = sb("xc_hi", [P, DC, P], F32R), sb("xc_lo", [P, DC, P], F32R)
        bo, bb = sb("bo", [P, D], F32), sb("bb", [P, D], F32)
        ident = sb("ident_c", [P, P], F32)
        stats, mv = sb("stats_c", [P, 2, 6], F32), sb("mv_c", [P, 2], F32)
        var, std, rstd = sb("var_c", [P, 1], F32), sb("std_c", [P, 1], F32), sb("rstd_c", [P, 1], F32)
        mk8 = sb("mk8", [P, DC, E, R], U8)
        four = [o_in[:, 0, k].rearrange("p c t -> p (c t)") for k in range(3)]
        w_in = [h1[:, 0, :], h1[:, 1, :], h_in[:, 1, :]]
        enc_sb = o_in[0:R, 1, 0].rearrange("p c t -> p (c t)")
        tw = o_in[0:R, 1, 1].rearrange("p c t -> p (c t)")
        by_expert = lambda a: a.rearrange("p (c e r) -> p c e r", e=E, r=R)
        cf = by_expert(h_in[:, 0, 0:DC * E * R])
        mkf = by_expert(o_in[:, 1, 2].rearrange("p c t -> p (c t)")[:, 0:DC * E * R])
        wr = xn[:, 0:DC * R].rearrange("p (c r) -> p c r", r=R)
        den = a_f[:].rearrange("p c t -> p (c t)")
        halves = lambda a: a.rearrange("h (a t) -> (h a) t", a=2)
        t2_ps = ctx.enter_context(nc.psum_tensor("t2_ps", [P, DC, P], F32))
        o_ps = ctx.enter_context(nc.psum_tensor("oc_ps", [P, D], F32))
        f_ps = ctx.enter_context(nc.psum_tensor("f_ps", [P, D], F32))
        delta_ps = (f_ps[:], t2_ps[:].rearrange("p c t -> p (c t)"))

        consts, coefs_in, four_in = sem("consts_c"), sem("coefs_in"), [sem(f"four_in{s}") for s in range(3)]
        den_loaded, den_inverted, recip_stored = sem("den_loaded"), sem("den_inverted"), sem("recip_stored")
        w_loaded = [sem(f"wc_loaded{s}") for s in range(3)]
        prep, tw_ps_done, tw_done = sem("prep"), sem("tw_ps_done"), sem("tw_done")
        delta_ready, wsum_done = sem("delta_ready"), sem("wsum_done")
        w_hi_done, w_lo_done = sem("wc_hi_done"), sem("wc_lo_done")
        o_loaded = [sem(f"o_loaded{s}") for s in range(2)]
        h_loaded = [sem(f"h_loaded{s}") for s in range(2)]
        a_sum, a_ready = sem("a_sum"), sem("a_ready")
        a_hi_done, a_lo_done = sem("a_hi_done"), sem("a_lo_done")
        hb_done, o_ready, h1_done, h1b_done = sem("hb_done"), sem("o_ready"), sem("h1_done"), sem("h1b_done")
        ln_step, var_ready, std_ready = sem("ln_step_c"), sem("var_ready_c"), sem("std_ready_c")
        xn_ready, t2_ready = sem("xn_ready_c"), sem("t2_ready")
        x_hi_done, x_lo_done, f_ready = sem("xc_hi_done"), sem("xc_lo_done"), sem("f_ready")
        out_done, dve_passed = sem("out_done"), sem("dve_passed_c")
        out_stored = [sem(f"out_stored{s}") for s in range(2)]
        EMPTY = 16
        ONE = 1
        NW = 2 * DC
        O_LOAD = 16 * (2 + P // HD)
        block = ctx.enter_context(nc.Block())

        def tiles(eng, tile):
            tile(0, 0, True, False)
            with eng.Fori(0, TILES // 2 - 1) as i:
                for k in range(2):
                    tile(2 * i + 1 + k, 1 - k, False, False)
            tile(TILES - 1, 1, False, True)

        def loads_of(t, s):
            return (t - s) // 2 + 1

        @block.sync
        def _(sp):
            for e in range(E):
                for dst, src in ((cf, coefs), (mk8[:], mask)):
                    sp.dma_start(dst[:, :, e], src[e].rearrange("(c p) r -> p c r", p=P)).then_inc(coefs_in, 16)

            def load_four(c):
                if c >= 3:
                    sp.wait_ge(tw_ps_done, c - 2)
                sp.dma_start(four[c % 3], fourier_t[c * P:(c + 1) * P, :]).then_inc(four_in[c % 3], 16)

            def load_w(n):
                if n >= 3:
                    sp.wait_ge(w_lo_done, n - 2)
                sp.dma_start(w_in[n % 3], (w_o_t, w_base_t)[n // DC][n % DC * P:(n % DC + 1) * P, :]
                             ).then_inc(w_loaded[n % 3], 16)

            load_four(0)
            sp.dma_start(den, halves(den_dram)).then_inc(den_loaded, 16)
            load_four(1)
            for n in range(2):
                load_w(n)
            load_four(2)
            sp.dma_start(enc_sb, enc).then_inc(consts, 16)
            sp.dma_start(ident[:], ident_in).then_inc(consts, 16)
            for dst, b in ((bo, b_o), (bb, b_base)):
                sp.dma_start(dst[:], b.rearrange("(a d) -> a d", a=1).broadcast_to([P, D])).then_inc(consts, 16)
            for c in range(3, DC):
                load_four(c)
                load_w(c - 1)
            sp.wait_ge(den_inverted, 1)
            sp.dma_start(halves(recip_dram), den).then_inc(recip_stored, 16)
            load_w(DC - 1)

            def load_h(t, s):
                sp.dma_start(h_in[:, s, :], h_dram[bass.ds(t * P, P), :]).then_inc(h_loaded[s], 16)

            def load_o(t, s):
                for r, src in enumerate((o_hi_dram, o_lo_dram)):
                    part = src[bass.ds((t // QT) * Q_DIM, Q_DIM), bass.ds((t % QT) * P, P)]
                    sp.dma_start(o_in[:, s, r], part.rearrange("(c p) t -> p c t", p=P)).then_inc(o_loaded[s], 16)
                part = recip_dram[bass.ds((t // QT) * HEADS, HEADS), bass.ds((t % QT) * P, P)]
                by_head = part.rearrange("(c j) t -> j c t", j=P // HD)
                for j in range(P // HD):
                    sp.dma_start(o_in[j * HD:(j + 1) * HD, s, 2], by_head[j:j + 1].broadcast_to([HD, DC, P])
                                 ).then_inc(o_loaded[s], 16)

            sp.wait_ge(tw_ps_done, DC)
            sp.wait_ge(recip_stored, 16)
            load_o(0, 0)
            load_h(0, 0)
            for n in range(DC, NW):
                load_w(n)
            sp.wait_ge(delta_ready, DC)
            load_o(1, 1)
            sp.wait_ge(w_lo_done, NW)
            load_h(1, 1)

            def tile(t, s, first, last):
                if not last:
                    sp.wait_ge(a_ready, t + 1)
                    load_o(t + 2, s)
                    sp.wait_ge(h1_done, t + 1)
                    load_h(t + 2, s)
                sp.wait_ge(out_done, t + 1 + ONE)
                sp.dma_start(out[bass.ds(t * P, P), :], h1[:, s, :]).then_inc(out_stored[s], 16)

            with sp.Fori(0, TILES // 2 - 1) as i:
                for s in range(2):
                    tile(2 * i + s, s, False, False)
            for s in range(2):
                tile(TILES - 2 + s, s, False, True)
            for s in range(2):
                sp.wait_ge(out_stored[s], EMPTY + 16 * TILES // 2)

        @block.gpsimd
        def _(pool):
            pool.wait_ge(consts, 64)

            def join(t, s, first):
                pool.wait_ge(o_loaded[s], O_LOAD * loads_of(t, s))
                if not first:
                    pool.wait_ge(a_lo_done, t)
                nc.gpsimd.tensor_tensor(a_f[:], o_in[:, s, 0], o_in[:, s, 1], ALU.add).then_inc(a_sum, 1)

            def tile(t, s, first, last):
                pool.wait_ge(h_loaded[s], 16 * loads_of(t, s))
                nc.gpsimd.tensor_tensor(h_in[:, s, :], h_in[:, s, :], bo[:], ALU.add).then_inc(hb_done, 1)
                if not last:
                    join(t + 1, 1 - s, False)
                pool.wait_ge(xn_ready, t + 1)
                nc.gpsimd.tensor_tensor(h1[:, s, :], h1[:, s, :], bb[:], ALU.add).then_inc(h1b_done, 1)

            join(0, 0, True)
            tiles(pool, tile)

        @block.scalar
        def _(act):
            for s in range(2):
                act.sem_inc(out_stored[s], EMPTY)
            for c in range(NW):
                l, k = c // DC, c % DC
                if l == 0:
                    act.wait_ge(w_loaded[c % 3], 16 * (c // 3 + 1))
                else:
                    act.wait_ge(wsum_done, k + 1)
                nc.scalar.copy(w_hi[:, l, k, :], w_in[c % 3]).then_inc(w_hi_done, 1)

            def a_high(t, first):
                act.wait_ge(a_ready, t + 1)
                if not first:
                    act.wait_ge(o_ready, t)
                nc.scalar.copy(a_hi[:], a_f[:]).then_inc(a_hi_done, 1)

            def tile(t, s, first, last):
                act.wait_ge(var_ready, t + 1)
                nc.scalar.activation(std[:], var[:], ACT.Sqrt).then_inc(std_ready, 1)
                if not last:
                    a_high(t + 1, False)
                act.wait_ge(t2_ready, t + 1)
                nc.scalar.copy(x_hi[:], t2_ps[:]).then_inc(x_hi_done, 1)

            a_high(0, True)
            tiles(act, tile)

        @block.vector
        def _(dve):
            dve.sem_inc(out_done, ONE)
            dve.wait_ge(coefs_in, 16 * 2 * E)
            step = Steps(dve, prep, 0)
            step.do(nc.vector.tensor_copy(mkf, mk8[:]))
            step.do(nc.vector.tensor_tensor(cf, cf, mkf, ALU.mult))
            step.do(nc.vector.tensor_tensor(wr, cf[:, :, 0, :], cf[:, :, 1, :], ALU.add))
            step.do(nc.vector.tensor_tensor(wr, wr, cf[:, :, 2, :], ALU.add))

            dve.wait_ge(den_loaded, 16)
            nc.vector.reciprocal(den, den).then_inc(den_inverted, 1)

            def w_low(c):
                dve.wait_ge(w_hi_done, c + 1)
                nc.vector.tensor_tensor(w_lo[:, c // DC, c % DC, :], w_in[c % 3],
                                        w_hi[:, c // DC, c % DC, :].bitcast(F32), ALU.subtract).then_inc(w_lo_done, 1)

            for c in range(DC):
                w_low(c)
            dve.wait_ge(tw_ps_done, DC)
            nc.vector.tensor_scalar(tw, o_ps[0:R, :], SCALING, None, ALU.mult).then_inc(tw_done, 1)
            for c in range(DC + 1):
                if c < DC:
                    n = DC + c
                    dve.wait_ge(w_loaded[n % 3], 16 * (n // 3 + 1))
                    dve.wait_ge(delta_ready, c + 1)
                    nc.vector.tensor_tensor(w_in[n % 3], w_in[n % 3], delta_ps[c % 2], ALU.add).then_inc(wsum_done, 1)
                if c >= 1:
                    w_low(DC + c - 1)
            LN_STEPS = 4

            def attended(t, s):
                dve.wait_ge(a_sum, t + 1)
                nc.vector.tensor_tensor(a_f[:], a_f[:], o_in[:, s, 2], ALU.mult).then_inc(a_ready, 1)

            def a_low(t):
                dve.wait_ge(a_hi_done, t + 1)
                nc.vector.tensor_tensor(a_lo[:], a_f[:], a_hi[:].bitcast(F32), ALU.subtract).then_inc(a_lo_done, 1)

            def finish(t, s):
                dve.wait_ge(f_ready, t + 1)
                dve.wait_ge(h1b_done, t + 1)
                nc.vector.tensor_tensor(h1[:, s, :], f_ps[:], h1[:, s, :], ALU.add).then_inc(out_done, 1)

            def tile(t, s, first, last):
                dve.wait_ge(o_ready, t + 1)
                dve.wait_ge(hb_done, t + 1)
                dve.wait_ge(out_stored[s], EMPTY + 16 * (loads_of(t, s) - 1))
                nc.vector.tensor_tensor(h1[:, s, :], o_ps[:], h_in[:, s, :], ALU.add).then_inc(h1_done, 1)
                dve.wait_ge(h1_done, t + 1)
                st = Steps(dve, ln_step, t * LN_STEPS)
                st.do(nc.vector.bn_stats(stats[:, 0, :], h1[:, s, 0:512]))
                st.do(nc.vector.bn_stats(stats[:, 1, :], h1[:, s, 512:1024]))
                pass_waits(dve, dve_passed)
                st.do(nc.vector.bn_aggr(mv[:], stats[:].rearrange("p a s -> p (a s)")))
                nc.vector.tensor_scalar(var[:], mv[:, 1:2], EPS, None, ALU.add).then_inc(var_ready, 1)
                dve.wait_ge(std_ready, t + 1)
                st.do(nc.vector.reciprocal(rstd[:], std[:]))
                if not first:
                    dve.wait_ge(t2_ready, t)
                nc.vector.tensor_scalar(xn[:], h1[:, s, :], mv[:, 0:1], rstd[:], ALU.subtract,
                                        ALU.mult).then_inc(xn_ready, 1)
                if not last:
                    attended(t + 1, 1 - s)
                    a_low(t + 1)
                if not first:
                    finish(t - 1, 1 - s)
                dve.wait_ge(x_hi_done, t + 1)
                nc.vector.tensor_tensor(x_lo[:], t2_ps[:], x_hi[:].bitcast(F32), ALU.subtract).then_inc(x_lo_done, 1)

            attended(0, 0)
            a_low(0)
            tiles(dve, tile)
            finish(TILES - 1, 1)

        @block.tensor
        def _(pe):
            pe.wait_ge(prep, 4)
            for c in range(DC):
                pe.wait_ge(four_in[c % 3], 16 * (c // 3 + 1))
                for n in range(2):
                    mm = nc.tensor.matmul(o_ps[0:R, n * 512:(n + 1) * 512], wr[:, c, :],
                                          four[c % 3][:, n * 512:(n + 1) * 512], start=(c == 0), stop=(c == DC - 1))
                mm.then_inc(tw_ps_done, 1)
            pe.wait_ge(tw_done, 1)
            pe.wait_ge(consts, 64)
            for c in range(DC):
                if c >= 2:
                    pe.wait_ge(wsum_done, c - 1)
                for n in range(2):
                    mm = nc.tensor.matmul(delta_ps[c % 2][:, n * 512:(n + 1) * 512], enc_sb[:, c * P:(c + 1) * P],
                                          tw[:, n * 512:(n + 1) * 512], start=True, stop=True)
                mm.then_inc(delta_ready, 1)
            pe.wait_ge(w_lo_done, NW)

            def turn_x(t, first):
                pe.wait_ge(xn_ready, t + 1)
                if not first:
                    pe.wait_ge(x_lo_done, t)
                for c in range(DC):
                    mm = nc.tensor.transpose(t2_ps[:, c, :], xn[:, c * P:(c + 1) * P], ident[:])
                mm.then_inc(t2_ready, 1)

            def product(out_ps, x, l, done):
                for c in range(DC):
                    for k, (a, b) in enumerate(((0, 0), (0, 1), (1, 0))):
                        for n in range(2):
                            mm = nc.tensor.matmul(out_ps[:, n * 512:(n + 1) * 512], x[a][:, c, :],
                                                  (w_hi, w_lo)[b][:, l, c, n * 512:(n + 1) * 512],
                                                  start=(c == 0 and k == 0), stop=(c == DC - 1 and k == 2))
                mm.then_inc(done, 1)

            def last_layer(t):
                pe.wait_ge(x_lo_done, t + 1)
                pe.wait_ge(out_done, t + ONE)
                product(f_ps, (x_hi, x_lo), 1, f_ready)

            def tile(t, s, first, last):
                pe.wait_ge(a_lo_done, t + 1)
                if not first:
                    pe.wait_ge(h1_done, t)
                product(o_ps, (a_hi, a_lo), 0, o_ready)
                if not first:
                    last_layer(t - 1)
                turn_x(t, first)

            tiles(pe, tile)
            last_layer(TILES - 1)


def build(nc, x_ctx, t0, t1, t2, t3, tok_b, w_qkv_t, b_qk, b_v, w_o_t, b_o, w_base_t, b_base, enc, coefs, mask,
          rope, fourier_t, ident, mask_qk, mask_kq, out):
    scratch = lambda n, s, d: nc.dram_tensor(n, s, d, kind="Internal").ap()
    h_dram = scratch("h_scratch", [TOKENS, D], F32)
    q_hi = scratch("q_hi_scratch", [BATCH * Q_DIM, SEQ], F32)
    q_lo = scratch("q_lo_scratch", [BATCH * Q_DIM, SEQ], F32)
    k_hi = scratch("k_hi_scratch", [BATCH * KV_DIM, SEQ], F32)
    k_lo = scratch("k_lo_scratch", [BATCH * KV_DIM, SEQ], F32)
    v_dram = scratch("v_scratch", [GROUPS, P, QT, VW], F32)
    o_hi_dram = scratch("o_hi_scratch", [BATCH * Q_DIM, SEQ], F32)
    o_lo_dram = scratch("o_lo_scratch", [BATCH * Q_DIM, SEQ], F32)
    den_dram = scratch("den_scratch", [ALL_HEADS, SEQ], F32)
    recip_dram = scratch("recip_scratch", [ALL_HEADS, SEQ], F32)
    part_a(nc, x_ctx, (t0, t1, t2, t3), tok_b, w_qkv_t, b_qk, b_v, rope, h_dram, q_hi, q_lo, k_hi, k_lo, v_dram, ident)
    part_b(nc, q_hi, q_lo, k_hi, k_lo, v_dram, o_hi_dram, o_lo_dram, den_dram, ident, mask_qk, mask_kq)
    part_c(nc, o_hi_dram, o_lo_dram, den_dram, recip_dram, h_dram, w_o_t, b_o, w_base_t, b_base, enc, coefs, mask,
           fourier_t, ident, out)


def rope_table():
    inv = (1.0 / np.float32(10000.0) ** (np.arange(0, HD, 2, dtype=np.float32) / np.float32(HD))).astype(np.float32)
    ang = np.arange(SEQ, dtype=np.float32)[:, None] * inv[None, :]
    cos, sin = np.cos(ang).T, np.sin(ang).T
    cos = np.repeat(cos, 2, axis=0)
    sin = np.stack([-sin, sin], axis=1).reshape(HD, SEQ)
    tab = np.tile(np.stack([cos, sin], axis=1), (P // HD, 1, 1))
    tab = tab.reshape(P, 2, QC, CT).transpose(2, 0, 1, 3)
    return np.ascontiguousarray(np.concatenate([tab] * BATCH)).astype(np.float32)


def fourier_matrix_t():
    n = D
    o = np.arange(n)
    rows = np.zeros((n, n))
    rows[0] = 1.0 / np.sqrt(n)
    f = np.arange(1, (n - 1) // 2 + 1)
    ang = 2.0 * np.pi * ((f[:, None] * o[None, :]) % n) / n
    rows[1:2 * len(f):2] = np.sqrt(2.0 / n) * np.cos(ang)
    rows[2:2 * len(f) + 1:2] = np.sqrt(2.0 / n) * np.sin(ang)
    rows[n - 1] = np.where(o % 2 == 0, 1.0, -1.0) / np.sqrt(n)
    return rows.astype(np.float32)


def kernel(**inputs):
    import concourse.bacc as _bacc
    from concourse.bass_utils import run_bass_kernel_spmd as _run

    a = {k: np.asarray(v) for k, v in inputs.items()}
    x = a["x"]
    ctx = [np.concatenate([np.full((BATCH, s), VOCAB, x.dtype), x[:, :SEQ - s]], axis=1) for s in (3, 2, 1, 0)]
    ctx = np.stack(ctx, axis=-1).reshape(CHUNKS, TPC, P, ORDER).transpose(2, 0, 1, 3).reshape(P, CHUNKS, TPC * ORDER)
    tok = a["L0_tok_W"].T.reshape(ORDER, VOCAB + 1, VOCAB)
    b_qkv = a["L0_attn_b_qkv"]
    order = np.arange(P)
    arrays = {"x_ctx": ctx}
    arrays.update({f"tok_table{k}": tok[k] for k in range(ORDER)})
    arrays.update({
        "tok_b": a["L0_tok_b"],
        "w_qkv_t": a["L0_attn_w_qkv"].T,
        "b_qk": b_qkv[:Q_DIM + KV_DIM].reshape(QK_TILES, P).T,
        "b_v": b_qkv[Q_DIM + KV_DIM:],
        "w_o_t": a["L0_attn_w_o"].T,
        "b_o": a["L0_attn_b_o"],
        "w_base_t": a["L0_ffn_W_base"].T,
        "b_base": a["L0_ffn_b_base"],
        "enc": np.concatenate([a["L0_ffn_enc0"], a["L0_ffn_enc1"]], axis=0),
        "coefs": np.concatenate([a["L0_ffn_coefs0"], a["L0_ffn_coefs1"]], axis=2),
        "mask": np.concatenate([a["L0_ffn_mask0"], a["L0_ffn_mask1"]], axis=2),
        "rope": rope_table(),
        "fourier_t": fourier_matrix_t(),
        "ident": np.eye(P, dtype=np.float32),
        "mask_qk": np.where(order[None, :] > order[:, None], MASKED, 0.0).astype(np.float32),
        "mask_kq": np.where(order[None, :] < order[:, None], MASKED, 0.0).astype(np.float32),
    })
    nc = _bacc.Bacc("TRN2", target_bir_lowering=False, num_devices=1)
    maps, args = {}, []
    for name, value in arrays.items():
        value = np.ascontiguousarray(value)
        maps[f"in_{name}"] = value
        args.append(nc.dram_tensor(f"in_{name}", value.shape, mybir.dt.from_np(value.dtype), kind="ExternalInput").ap())
    args.append(nc.dram_tensor("out_dram", (TOKENS, D), F32, kind="ExternalOutput").ap())
    build(nc, *args)
    r = _run(nc, [maps], core_ids=[0])
    return r.results[0]["out_dram"].reshape(BATCH, SEQ, D)
```
